# Optimizing a Trainium2 kernel written in Bass

```python
import numpy as np
import jax
import jax.numpy as jnp

def _softmax(x, axis=-1):
    return jax.nn.softmax(x, axis=axis)

def _gelu(x):
    return jax.nn.gelu(x, approximate=True)

def _silu(x):
    return jax.nn.silu(x)

def _sigmoid(x):
    return jax.nn.sigmoid(x)

def _layernorm(x, axis=-1, eps=1e-05):
    m = jnp.mean(x, axis=axis, keepdims=True)
    v = jnp.var(x, axis=axis, keepdims=True)
    return (x - m) / jnp.sqrt(v + eps)

def _scatter_add(tgt, idx, src, axis=0):
    return tgt.at[idx].add(src)

def _segment_sum(src, seg, n):
    return jax.ops.segment_sum(src, seg, n)
kernel_name = 'mk_seq_postln_d1_jaxref_r4_5918de'

def setup_inputs(seed: int=0):
    np.random.seed(seed)
    _w = jnp.asarray

    def _L0_attn_setup():
        import jax, jax.numpy as jnp
        import numpy as np

        def _mamba_fwd(hidden_states, in_proj_w, conv_w, conv_b, x_proj_w, dt_proj_w, dt_proj_b, A_log, D_param, out_proj_w):
            Bsz, L, _ = hidden_states.shape
            d_inner = conv_w.shape[0]
            n = A_log.shape[1]
            r = dt_proj_w.shape[1]
            xz = jnp.einsum('bld,ed->ble', hidden_states, in_proj_w)
            x, z = (xz[..., :d_inner], xz[..., d_inner:])
            x_bdl = jnp.transpose(x, (0, 2, 1))
            kern = conv_w[:, None, :]
            xc = jax.lax.conv_general_dilated(x_bdl, kern, window_strides=(1,), padding=[(conv_w.shape[1] - 1, 0)], dimension_numbers=('NCH', 'OIH', 'NCH'), feature_group_count=d_inner)
            xc = xc + conv_b[None, :, None]
            xc = xc * jax.nn.sigmoid(xc)
            u = jnp.transpose(xc, (0, 2, 1))
            x_dbl = jnp.einsum('bld,ed->ble', u, x_proj_w)
            dt_lo = x_dbl[..., :r]
            B_ssm = x_dbl[..., r:r + n]
            C_ssm = x_dbl[..., r + n:]
            delta = jax.nn.softplus(jnp.einsum('blr,dr->bld', dt_lo, dt_proj_w) + dt_proj_b)
            A = -jnp.exp(A_log)

            def step(h, inp):
                d_t, u_t, b_t, c_t = inp
                dA = jnp.exp(d_t[..., None] * A)
                h = dA * h + (d_t * u_t)[..., None] * b_t[:, None, :]
                y_t = jnp.einsum('bdn,bn->bd', h, c_t)
                return (h, y_t)
            h0 = jnp.zeros((Bsz, d_inner, n), dtype=u.dtype)
            xs = (jnp.transpose(delta, (1, 0, 2)), jnp.transpose(u, (1, 0, 2)), jnp.transpose(B_ssm, (1, 0, 2)), jnp.transpose(C_ssm, (1, 0, 2)))
            _, ys = jax.lax.scan(step, h0, xs)
            y = jnp.transpose(ys, (1, 0, 2)) + u * D_param
            y = y * (z * jax.nn.sigmoid(z))
            return jnp.einsum('bld,ed->ble', y, out_proj_w)
        key = jax.random.key(seed)
        ks = jax.random.split(key, 10)
        B, L, D_MODEL = (2, 512, 256)
        D_INNER, N, W, R = (512, 16, 4, 64)
        s = 0.02
        return {'hidden_states': jax.random.normal(ks[0], (B, L, D_MODEL), jnp.float32), 'in_proj_w': jax.random.normal(ks[1], (2 * D_INNER, D_MODEL), jnp.float32) * s, 'conv_w': jax.random.normal(ks[2], (D_INNER, W), jnp.float32) * 0.2, 'conv_b': jax.random.normal(ks[3], (D_INNER,), jnp.float32) * 0.02, 'x_proj_w': jax.random.normal(ks[4], (R + 2 * N, D_INNER), jnp.float32) * s, 'dt_proj_w': jax.random.normal(ks[5], (D_INNER, R), jnp.float32) * R ** (-0.5), 'dt_proj_b': jnp.log(jnp.expm1(jnp.exp(jax.random.uniform(ks[6], (D_INNER,), jnp.float32, np.log(0.001), np.log(0.1)))) + 1e-20), 'A_log': jnp.log(jnp.broadcast_to(jnp.arange(1, N + 1, dtype=jnp.float32), (D_INNER, N))), 'D_param': jnp.ones((D_INNER,), jnp.float32), 'out_proj_w': jax.random.normal(ks[7], (D_MODEL, D_INNER), jnp.float32) * s}
    _L0_attn_in = _L0_attn_setup()

    def _L0_ffn_setup():
        import jax, jax.numpy as jnp
        import numpy as np
        D_IN, D_HID = (256, 1024)

        def _ternary(key, shape):
            return jax.random.randint(key, shape, -1, 2).astype(jnp.float32)

        def _tlin(x, w, s):
            return jnp.einsum('bsi,oi->bso', x, w) * s
        key = jax.random.key(seed)
        ks = jax.random.split(key, 12)
        inv = lambda fan: 1.0 / np.sqrt(fan).astype(np.float32)
        return {'x': jax.random.normal(ks[0], (4, 512, D_IN), dtype=jnp.float32), 'w1_w': _ternary(ks[1], (D_HID, D_IN)), 'w1_s': jax.random.uniform(ks[2], (D_HID,), dtype=jnp.float32) * inv(D_IN), 'w2_w': _ternary(ks[3], (D_HID, D_IN)), 'w2_s': jax.random.uniform(ks[4], (D_HID,), dtype=jnp.float32) * inv(D_IN), 'h1_w': _ternary(ks[5], (D_HID, D_HID)), 'h1_s': jax.random.uniform(ks[6], (D_HID,), dtype=jnp.float32) * inv(D_HID), 'h2_w': _ternary(ks[7], (D_HID, D_HID)), 'h2_s': jax.random.uniform(ks[8], (D_HID,), dtype=jnp.float32) * inv(D_HID), 'w3_w': _ternary(ks[9], (D_IN, D_HID)), 'w3_s': jax.random.uniform(ks[10], (D_IN,), dtype=jnp.float32) * inv(D_HID)}
    _L0_ffn_in = _L0_ffn_setup()
    _d = {'L0_attn_hidden_states': _L0_attn_in['hidden_states'], 'L0_attn_in_proj_w': _L0_attn_in['in_proj_w'], 'L0_attn_conv_w': _L0_attn_in['conv_w'], 'L0_attn_conv_b': _L0_attn_in['conv_b'], 'L0_attn_x_proj_w': _L0_attn_in['x_proj_w'], 'L0_attn_dt_proj_w': _L0_attn_in['dt_proj_w'], 'L0_attn_dt_proj_b': _L0_attn_in['dt_proj_b'], 'L0_attn_A_log': _L0_attn_in['A_log'], 'L0_attn_D_param': _L0_attn_in['D_param'], 'L0_attn_out_proj_w': _L0_attn_in['out_proj_w'], 'L0_ffn_w1_w': _L0_ffn_in['w1_w'], 'L0_ffn_w1_s': _L0_ffn_in['w1_s'], 'L0_ffn_w2_w': _L0_ffn_in['w2_w'], 'L0_ffn_w2_s': _L0_ffn_in['w2_s'], 'L0_ffn_h1_w': _L0_ffn_in['h1_w'], 'L0_ffn_h1_s': _L0_ffn_in['h1_s'], 'L0_ffn_h2_w': _L0_ffn_in['h2_w'], 'L0_ffn_h2_s': _L0_ffn_in['h2_s'], 'L0_ffn_w3_w': _L0_ffn_in['w3_w'], 'L0_ffn_w3_s': _L0_ffn_in['w3_s']}
    _x0 = _d['L0_attn_hidden_states']
    _d['L0_attn_hidden_states'] = jax.random.normal(jax.random.fold_in(jax.random.key(seed), 1), (4, 2048, 256), dtype=_x0.dtype)
    del _x0
    return _d

def reference(L0_attn_hidden_states, L0_attn_in_proj_w, L0_attn_conv_w, L0_attn_conv_b, L0_attn_x_proj_w, L0_attn_dt_proj_w, L0_attn_dt_proj_b, L0_attn_A_log, L0_attn_D_param, L0_attn_out_proj_w, L0_ffn_w1_w, L0_ffn_w1_s, L0_ffn_w2_w, L0_ffn_w2_s, L0_ffn_h1_w, L0_ffn_h1_s, L0_ffn_h2_w, L0_ffn_h2_s, L0_ffn_w3_w, L0_ffn_w3_s):

    def _L0_attn_ref(hidden_states, in_proj_w, conv_w, conv_b, x_proj_w, dt_proj_w, dt_proj_b, A_log, D_param, out_proj_w):
        import jax, jax.numpy as jnp
        import numpy as np

        def _mamba_fwd(hidden_states, in_proj_w, conv_w, conv_b, x_proj_w, dt_proj_w, dt_proj_b, A_log, D_param, out_proj_w):
            Bsz, L, _ = hidden_states.shape
            d_inner = conv_w.shape[0]
            n = A_log.shape[1]
            r = dt_proj_w.shape[1]
            xz = jnp.einsum('bld,ed->ble', hidden_states, in_proj_w)
            x, z = (xz[..., :d_inner], xz[..., d_inner:])
            x_bdl = jnp.transpose(x, (0, 2, 1))
            kern = conv_w[:, None, :]
            xc = jax.lax.conv_general_dilated(x_bdl, kern, window_strides=(1,), padding=[(conv_w.shape[1] - 1, 0)], dimension_numbers=('NCH', 'OIH', 'NCH'), feature_group_count=d_inner)
            xc = xc + conv_b[None, :, None]
            xc = xc * jax.nn.sigmoid(xc)
            u = jnp.transpose(xc, (0, 2, 1))
            x_dbl = jnp.einsum('bld,ed->ble', u, x_proj_w)
            dt_lo = x_dbl[..., :r]
            B_ssm = x_dbl[..., r:r + n]
            C_ssm = x_dbl[..., r + n:]
            delta = jax.nn.softplus(jnp.einsum('blr,dr->bld', dt_lo, dt_proj_w) + dt_proj_b)
            A = -jnp.exp(A_log)

            def step(h, inp):
                d_t, u_t, b_t, c_t = inp
                dA = jnp.exp(d_t[..., None] * A)
                h = dA * h + (d_t * u_t)[..., None] * b_t[:, None, :]
                y_t = jnp.einsum('bdn,bn->bd', h, c_t)
                return (h, y_t)
            h0 = jnp.zeros((Bsz, d_inner, n), dtype=u.dtype)
            xs = (jnp.transpose(delta, (1, 0, 2)), jnp.transpose(u, (1, 0, 2)), jnp.transpose(B_ssm, (1, 0, 2)), jnp.transpose(C_ssm, (1, 0, 2)))
            _, ys = jax.lax.scan(step, h0, xs)
            y = jnp.transpose(ys, (1, 0, 2)) + u * D_param
            y = y * (z * jax.nn.sigmoid(z))
            return jnp.einsum('bld,ed->ble', y, out_proj_w)
        return _mamba_fwd(hidden_states, in_proj_w, conv_w, conv_b, x_proj_w, dt_proj_w, dt_proj_b, A_log, D_param, out_proj_w)

    def _L0_ffn_ref(x, w1_w, w1_s, w2_w, w2_s, h1_w, h1_s, h2_w, h2_s, w3_w, w3_s):
        import jax, jax.numpy as jnp
        import numpy as np
        D_IN, D_HID = (256, 1024)

        def _ternary(key, shape):
            return jax.random.randint(key, shape, -1, 2).astype(jnp.float32)

        def _tlin(x, w, s):
            return jnp.einsum('bsi,oi->bso', x, w) * s
        h = jax.nn.silu(_tlin(x, w1_w, w1_s)) * _tlin(x, w2_w, w2_s)
        h = jax.nn.gelu(_tlin(h, h1_w, h1_s), approximate=False)
        h = jax.nn.gelu(_tlin(h, h2_w, h2_s), approximate=False)
        return _tlin(h, w3_w, w3_s)
    x = L0_attn_hidden_states
    x = _layernorm(x + _L0_attn_ref(x, L0_attn_in_proj_w, L0_attn_conv_w, L0_attn_conv_b, L0_attn_x_proj_w, L0_attn_dt_proj_w, L0_attn_dt_proj_b, L0_attn_A_log, L0_attn_D_param, L0_attn_out_proj_w), axis=-1)
    x = _layernorm(x + _L0_ffn_ref(x, L0_ffn_w1_w, L0_ffn_w1_s, L0_ffn_w2_w, L0_ffn_w2_s, L0_ffn_h1_w, L0_ffn_h1_s, L0_ffn_h2_w, L0_ffn_h2_s, L0_ffn_w3_w, L0_ffn_w3_s), axis=-1)
    return x

_drawn_inputs = setup_inputs


def setup_inputs(seed=0):
    import zlib

    import numpy as np

    out = dict(_drawn_inputs(seed))
    spreads = {'L0_attn_D_param': (1.0, 0.6)}
    factors = {'L0_attn_in_proj_w': 8.0,
     'L0_attn_conv_w': 8.0,
     'L0_attn_conv_b': 8.0,
     'L0_attn_x_proj_w': 8.0,
     'L0_attn_dt_proj_w': 8.0,
     'L0_attn_dt_proj_b': 8.0,
     'L0_attn_A_log': 8.0,
     'L0_attn_out_proj_w': 8.0,
     'L0_ffn_w1_w': 8.0,
     'L0_ffn_w1_s': 8.0,
     'L0_ffn_w2_w': 8.0,
     'L0_ffn_w2_s': 8.0,
     'L0_ffn_h1_w': 8.0,
     'L0_ffn_h1_s': 8.0,
     'L0_ffn_h2_w': 8.0,
     'L0_ffn_h2_s': 8.0,
     'L0_ffn_w3_w': 8.0,
     'L0_ffn_w3_s': 8.0}
    for name, (base, spread) in spreads.items():
        noise = np.random.default_rng([zlib.crc32(name.encode()), seed]).standard_normal(out[name].shape)
        drawn = base * np.exp(spread * noise) if base else spread * noise
        out[name] = jnp.asarray(drawn.astype(out[name].dtype))
    for name, factor in factors.items():
        out[name] = (out[name] * factor).astype(out[name].dtype)
    return out
```

```python
import concourse.bass as bass
from concourse import mybir
from contextlib import ExitStack
import numpy as np

F32 = mybir.dt.float32
F32R = mybir.dt.float32r
I32 = mybir.dt.int32
ALU = mybir.AluOpType
ACT = mybir.ActivationFunctionType

P = 128
BATCH, SEQ, DM = 4, 2048, 256
DI, NS, DTR, TAPS = 512, 16, 64, 4
DH = 1024
NT = 512
TILES_B = SEQ // NT
TILES = BATCH * TILES_B
KM, KI, KH = DM // P, DI // P, DH // P
SUB = NT // P
GD = P // NS
NG = DI // GD
GC = P // GD
QUADS = NG // 4
HALF = P // 2
HRING = 8
EPS = 1e-5
EXP_LN = "natural_log_exp_and_others"
RSQRT_SEED = float(0x5F3759DF)


def group_place(g):
    chunk, k = divmod(g, GC)
    quadrant, step = k % 4, k // 4
    return chunk, quadrant, step


class Tile:

    def __init__(self, b, tt):
        self.b, self.tt = b, tt

    def count(self, per_tile, n):
        return self.b * (self.OF_STEP * per_tile) + (self.tt * per_tile + n)

    def following(self):
        if self.tt + 1 < self.OF_STEP:
            return type(self)(self.b, self.tt + 1)
        return type(self)(self.b + 1, 0)


class SeqTile(Tile):
    OF_STEP = TILES_B


class PairTile(Tile):
    OF_STEP = 2


Z_FROM, CONV_FROM, PRODUCTS = KI * KM, 2 * KI * KM, 2 * KI * KM + KI * TAPS
SILU_SLOT, XD_SLOT, ROWS_SLOT, DT_SLOTS = 27, 29, 34, (36, 41, 46, 51)
FRONT_SLOTS = 61


def products_of(slot):
    return range(min(slot * 5 // 4, PRODUCTS), min((slot + 1) * 5 // 4, PRODUCTS))


def slot_after(product):
    return product * 4 // 5 + 1 + (product * 4 % 5 > 0 and product not in products_of(product * 4 // 5))


def d_bank(g):
    return g % 3 if g < NG - 1 else 1


def d_bank_before(g):
    return 2 if g in (1, NG - 1) else 3


OPENING = SeqTile(0, 0)
PAST = SeqTile(BATCH, 0)


def rstd_newton(dve, link, var4, y4, a4):
    link(dve.tensor_scalar(var4[:], var4[:], EPS, None, ALU.add))
    link(dve.tensor_scalar(a4[:].bitcast(I32), var4[:].bitcast(I32), 1, None, ALU.logical_shift_right))
    link(dve.tensor_scalar(y4[:].bitcast(I32), a4[:].bitcast(I32), -1.0, RSQRT_SEED, ALU.mult, ALU.add))
    for _ in range(4):
        link(dve.tensor_tensor(a4[:], y4[:], y4[:], ALU.mult))
        link(dve.tensor_tensor(a4[:], a4[:], var4[:], ALU.mult))
        link(dve.tensor_scalar(a4[:], a4[:], -0.5, 1.5, ALU.mult, ALU.add))
        link(dve.tensor_tensor(y4[:], y4[:], a4[:], ALU.mult))


def mamba_stage(nc, sems, xT, x, in_wT, conv_w, conv_b, xp_wT, dt_wT, dt_b, A_log, D_param, out_wT,
                pick, fold, ident, x1):
    ctx = ExitStack()
    with ctx:
        def sb(name, shape, dt=F32):
            return ctx.enter_context(nc.sbuf_tensor(name, shape, dt))

        def sem(name):
            return sems.enter_context(nc.semaphore(name))

        w_in = sb("w_in", [P, KM, 2 * DI])
        w_xp = sb("w_xp", [P, KI, DTR + 2 * NS])
        w_dt = sb("w_dt", [DTR, DI])
        w_out = sb("w_out", [P, KI, DM])
        w_conv = sb("w_conv", [P, KI, TAPS, P])
        pick_r = sb("pick_r", [P, HALF // GD, P], F32R)
        fold_w = sb("fold_w", [P, 4, 32])
        spread_bc = sb("spread_bc", [P, 2, P])
        taps = sb("taps", [P, KI, TAPS])
        cb = sb("cb", [P, KI])
        dtb = sb("dtb", [P, KI])
        dpar = sb("dpar", [P, KI])
        a_neg = sb("a_neg", [P, NG])
        zeros = sb("zeros", [P, NG])
        xT_sb = sb("xT_sb", [P, KM, NT])
        x_nat = sb("x_nat", [P, SUB, DM])
        res = sb("res", [P, SUB, DM])
        xb = sb("xb", [P, KI, TAPS - 1 + NT])
        uz = [sb(f"uz{i}", [P, 2 * KI, NT]) for i in range(2)]
        d_parts = [sb(f"d_parts{i}", [P, 2, KI, NT], F32R) for i in range(2)]
        du_parts = [sb(f"du_parts{i}", [P, 2, KI, NT], F32R) for i in range(2)]
        b_rows = [sb(f"b_rows{i}", [P, NT]) for i in range(2)]
        c_rows = [sb(f"c_rows{i}", [P, NT]) for i in range(2)]
        sp_e = [sb(f"sp_e{i}", [P, NT]) for i in range(2)]
        sp_w = [sb(f"sp_w{i}", [P, NT]) for i in range(2)]
        sp_l = sb("sp_l", [P, NT])
        sp_r = [sb(f"sp_r{i}", [P, NT]) for i in range(2)]
        db = [sb(f"db{i}", [P, NT]) for i in range(2)]
        h = sb("h", [P, HRING, NT])
        hc = sb("hc", [P, HRING, NT])
        state = sb("state", [P, NG])
        stats = sb("stats", [P, SUB, 6])
        mv = sb("mv", [P, SUB, 2])
        var4 = sb("var4", [P, SUB])
        y4 = sb("y4", [P, SUB])
        a4 = sb("a4", [P, SUB])
        xd = sb("xd", [DTR + 2 * NS, NT])

        bank = [ctx.enter_context(nc.psum_tensor(f"bank{i}", [P, NT], F32)) for i in range(8)]
        p_mm, p_d, p_du, p_y = bank[0:2], bank[2:5], bank[5:7], bank[7]

        weights_in = sem("weights_in")
        zeroed = sem("zeroed")
        a_exp = sem("a_exp")
        consts = sem("consts")
        xT_in, x_in, x1_out = sem("xT_in"), sem("x_in"), sem("x1_out")
        x_mm, z_mm, conv_mm, xd_mm, rows_mm, dt_mm, out_mm = (
            sem(s) for s in ("x_mm", "z_mm", "conv_mm", "xd_mm", "rows_mm", "dt_mm", "out_mm"))
        x_sb, z_sb, conv_sb, xd_sb, rows_sb, dt_sb, out_sb = (
            sem(s) for s in ("x_sb", "z_sb", "conv_sb", "xd_sb", "rows_sb", "dt_sb", "out_sb"))
        halo, silu = sem("halo"), sem("silu")
        sp_act = sem("sp_act")
        sp_dve = sem("sp_dve")
        d_hi, d_lo, du, du_hi, du_lo = (sem(s) for s in ("d_hi", "d_lo", "du", "du_hi", "du_lo"))
        d_bc, du_bc = sem("d_bc"), sem("du_bc")
        decay = sem("decay")
        dub = sem("dub")
        scanned = sem("scanned")
        saved = sem("saved")
        hc_done = sem("hc_done")
        folded = sem("folded")
        y_sb, gated = sem("y_sb"), sem("gated")
        ln_dve, ln_out = sem("ln_dve"), sem("ln_out")
        waited = sem("waited")

        block = ctx.enter_context(nc.Block())

        WEIGHTS = 12

        @block.sync
        def _(sp):
            for dst, src in (
                (w_in[:], in_wT.rearrange("(k p) e -> p k e", p=P)),
                (w_xp[:], xp_wT.rearrange("(k p) e -> p k e", p=P)),
                (w_dt[:], dt_wT),
                (w_out[:], out_wT.rearrange("(k p) e -> p k e", p=P)),
                (taps[:], conv_w.rearrange("(k p) w -> p k w", p=P)),
                (cb[:], conv_b),
                (dtb[:], dt_b),
                (dpar[:], D_param),
                (a_neg[:], A_log),
                (fold_w[:], fold),
                (uz[1][:, 0:2, :].rearrange("p a (g m) -> p (a g) m", m=P), pick),
                (uz[1][:, 2, 0:3 * P].rearrange("p (a m) -> p a m", m=P), ident),
            ):
                sp.dma_start(dst, src).then_inc(weights_in, 16)

            def load_xT(t):
                row = t.b if isinstance(t.b, int) else t.b % BATCH
                sp.dma_start(xT_sb[:], xT[row, :, t.tt * NT:(t.tt + 1) * NT]
                             .rearrange("(k p) t -> p k t", p=P)).then_inc(xT_in, 16)

            load_xT(OPENING)
            with sp.Fori(0, BATCH) as b:
                for tt in range(TILES_B):
                    t = SeqTile(b, tt)
                    nxt = t.following()
                    sp.wait_ge(z_mm, t.count(KI, KI))
                    sp.sem_inc(waited, 1)
                    load_xT(nxt)
                    sp.wait_ge(out_sb, t.count(SUB, 1))
                    sp.sem_inc(waited, 1)
                    sp.dma_start(x_nat[:], x[b, tt * NT:(tt + 1) * NT, :]
                                 .rearrange("(s p) c -> p s c", p=P)).then_inc(x_in, 16)
                    sp.wait_ge(ln_out, t.count(SUB, SUB))
                    sp.sem_inc(waited, 1)
                    sp.dma_start(x1[b, tt * NT:(tt + 1) * NT, :]
                                 .rearrange("(s p) c -> p s c", p=P), res[:]).then_inc(x1_out, 16)
            sp.wait_ge(x1_out, 16 * TILES + 16)

        @block.tensor
        def _(pe):
            pe.wait_ge(weights_in, 16 * WEIGHTS)
            pe.wait_ge(consts, 2)
            pe.sem_inc(folded, 2)

            def x_product(t, j, k):
                if k == 0:
                    if j == 0:
                        pe.wait_ge(xT_in, t.count(16, 16))
                    if j >= 2:
                        pe.wait_ge(x_sb, t.count(KI, j - 1))
                    elif t is not OPENING:
                        pe.wait_ge(out_sb, SeqTile(t.b, t.tt - 1).count(SUB, 1))
                last = pe.matmul(p_mm[j % 2][:], w_in[:, k, j * P:(j + 1) * P], xT_sb[:, k, :],
                                 start=k == 0, stop=k == KM - 1)
                if k == KM - 1:
                    last.then_inc(x_mm, 1)

            def z_product(t, j, k):
                if k == 0:
                    if j < 2:
                        pe.wait_ge(x_sb, t.count(KI, j + 3))
                    else:
                        pe.wait_ge(z_sb, t.count(KI, j - 1))
                last = pe.matmul(p_mm[j % 2][:], w_in[:, k, DI + j * P:DI + (j + 1) * P], xT_sb[:, k, :],
                                 start=k == 0, stop=k == KM - 1)
                if k == KM - 1:
                    last.then_inc(z_mm, 1)

            def conv_product(t, j, k):
                if k == 0:
                    if j < 2:
                        pe.wait_ge(z_sb, t.count(KI, j + 3))
                    else:
                        pe.wait_ge(conv_sb, t.count(KI, j - 1))
                last = pe.matmul(p_mm[j % 2][:], w_conv[:, j, k, :], xb[:, j, k:k + NT],
                                 start=k == 0, stop=k == TAPS - 1)
                if k == TAPS - 1:
                    last.then_inc(conv_mm, 1)

            def front(t, i):
                par = t.tt % 2
                for n in products_of(i):
                    if n < Z_FROM:
                        x_product(t, *divmod(n, KM))
                    elif n < CONV_FROM:
                        z_product(t, *divmod(n - Z_FROM, KM))
                    else:
                        conv_product(t, *divmod(n - CONV_FROM, TAPS))
                if XD_SLOT <= i < XD_SLOT + KI:
                    k = i - XD_SLOT
                    if k == 0:
                        pe.wait_ge(conv_sb, t.count(KI, KI - 1))
                        pe.wait_ge(silu, t.count(1, 1))
                    last = pe.matmul(p_mm[0][0:DTR + 2 * NS, :], w_xp[:, k, :], uz[par][:, k, :],
                                     start=k == 0, stop=k == KI - 1)
                    if k == KI - 1:
                        last.then_inc(xd_mm, 1)
                elif i == ROWS_SLOT:
                    pe.wait_ge(conv_sb, t.count(KI, KI))
                    pe.wait_ge(xd_sb, t.count(1, 1))
                    for m in range(2):
                        pe.matmul(p_mm[1 - m][:], spread_bc[DTR:DTR + 2 * NS, m, :],
                                  xd[DTR:DTR + 2 * NS, :], start=True, stop=True).then_inc(rows_mm, 1)
                elif i in DT_SLOTS:
                    c = DT_SLOTS.index(i)
                    if c < 2:
                        pe.wait_ge(rows_sb, t.count(2, c + 1))
                    else:
                        pe.wait_ge(dt_sb, t.count(KI, c - 1))
                    pe.matmul(p_mm[1 - c % 2][:], w_dt[:, c * P:(c + 1) * P], xd[0:DTR, :],
                              start=True, stop=True).then_inc(dt_mm, 1)

            def spread(t, g):
                chunk, quadrant, step = group_place(g)
                par, half = t.tt % 2, quadrant // 2
                which = (quadrant % 2) * 4 + step
                if quadrant % 4 == 0 and step == 0:
                    pe.wait_ge(d_lo, t.count(2 * KI, 2 * chunk + 2))
                    pe.wait_ge(du_lo, t.count(2 * KI, 2 * chunk + 2))
                pe.wait_ge(dub, t.count(NG, g + 1))
                pe.matmul(p_du[g % 2][:], pick_r[:, which, :], du_parts[par][:, half, chunk, :],
                          start=True, stop=True).then_inc(du_bc, 1)
                back = d_bank_before(g)
                if t is not OPENING or g + 3 - back > 0:
                    pe.wait_ge(scanned, t.count(NG, g + 3 - back))
                pe.matmul(p_d[d_bank(g)][:], pick_r[:, which, :], d_parts[par][:, half, chunk, :],
                          start=True, stop=True).then_inc(d_bc, 1)

            def fold_quad(t, q):
                chunk, step = divmod(q, 4)
                if step == 0:
                    pe.wait_ge(y_sb, t.count(KI, chunk + 1))
                pe.wait_ge(hc_done, t.count(NG, 4 * q + 4 + HRING))
                for k in range(4):
                    last = pe.matmul(p_y[32 * k:32 * k + 32, :], fold_w[:, step, :],
                                     hc[:, (4 * q + k) % HRING, :], start=step == 0, stop=step == 3,
                                     tile_position=(0, 32 * k))
                last.then_inc(folded, 1)

            def project(t, s):
                if s == 0:
                    pe.wait_ge(gated, t.count(KI, KI))
                if s < 2:
                    pe.wait_ge(dt_sb, t.following().count(KI, KI))
                else:
                    pe.wait_ge(out_sb, t.count(SUB, s))
                zs = uz[t.tt % 2]
                for k in range(KI):
                    last = pe.matmul(p_mm[s % 2][:, 0:DM], zs[:, KI + k, s * P:(s + 1) * P],
                                     w_out[:, k, :], start=k == 0, stop=k == KI - 1)
                last.then_inc(out_mm, 1)

            for i in range(FRONT_SLOTS):
                front(OPENING, i)
            for g in range(GC):
                spread(OPENING, g)
                if g % 4 == 1 and g > 5:
                    fold_quad(OPENING, g // 4 - 2)
            with pe.Fori(0, BATCH) as b:
                for tt in range(TILES_B):
                    t = SeqTile(b, tt)
                    nxt = t.following()
                    for i in range(NG):
                        now, g = (t, i + GC) if i < NG - GC else (nxt, i + GC - NG)
                        spread(now, g)
                        front(nxt, i)
                        if 58 <= i < 62:
                            project(t, i - 58)
                        if g % 4 == 1:
                            fold_quad(*((now, g // 4 - 2) if g > 5 else (t, g // 4 - 2 + QUADS)))
            fold_quad(PAST, 2)
            fold_quad(PAST, 3)

        @block.scalar
        def _(act):
            act.wait_ge(weights_in, 16 * WEIGHTS)
            act.preload_act_table_set(EXP_LN)
            act.activation(a_neg[:], a_neg[:], ACT.Exp).then_inc(a_exp, 1)
            act.wait_ge(consts, 2)
            act.wait_ge(zeroed, 1)
            act.activation(state[:], zeros[:], ACT.Copy).then_inc(saved, 16)

            def front(t, i):
                par = t.tt % 2
                if i == 0:
                    if t.tt == 0:
                        if t is not OPENING:
                            act.wait_ge(conv_mm, SeqTile(t.b, -1).count(KI, KI))
                        act.activation(xb[:, :, 0:TAPS - 1],
                                       zeros[:, 0:KI * (TAPS - 1)].rearrange("p (k w) -> p k w", k=KI),
                                       ACT.Copy).then_inc(halo, 1)
                    else:
                        act.wait_ge(conv_mm, SeqTile(t.b, t.tt - 1).count(KI, KI))
                        act.wait_ge(x_sb, SeqTile(t.b, t.tt - 1).count(KI, KI))
                        act.activation(xb[:, :, 0:TAPS - 1], xb[:, :, NT:NT + TAPS - 1],
                                       ACT.Copy).then_inc(halo, 1)
                for j in range(KI):
                    if i == slot_after(KM * j + KM - 1):
                        act.wait_ge(halo, t.count(1, 1))
                        act.wait_ge(x_mm, t.count(KI, j + 1))
                        act.activation(xb[:, j, TAPS - 1:], p_mm[j % 2][:], ACT.Copy).then_inc(x_sb, 1)
                    if i == slot_after(Z_FROM + KM * j + KM - 1):
                        act.wait_ge(z_mm, t.count(KI, j + 1))
                        act.activation(uz[par][:, KI + j, :], p_mm[j % 2][:], ACT.Copy).then_inc(z_sb, 1)
                    if i == slot_after(CONV_FROM + TAPS * j + TAPS - 1):
                        act.wait_ge(conv_mm, t.count(KI, j + 1))
                        act.activation(uz[par][:, j, :], p_mm[j % 2][:], ACT.Identity,
                                       bias=cb[:, j:j + 1]).then_inc(conv_sb, 1)
                if i == SILU_SLOT:
                    act.wait_ge(z_sb, t.count(KI, KI))
                    act.wait_ge(conv_sb, t.count(KI, KI))
                    act.activation(uz[par][:], uz[par][:], ACT.Silu).then_inc(silu, 1)
                    act.preload_act_table_set(EXP_LN)
                elif i == XD_SLOT + KI:
                    act.wait_ge(xd_mm, t.count(1, 1))
                    act.activation(xd[:], p_mm[0][0:DTR + 2 * NS, :], ACT.Copy).then_inc(xd_sb, 1)
                elif i == ROWS_SLOT + 1:
                    for m, rows in enumerate((b_rows, c_rows)):
                        act.wait_ge(rows_mm, t.count(2, m + 1))
                        act.activation(rows[par][:], p_mm[1 - m][:], ACT.Copy).then_inc(rows_sb, 1)
                for c in range(KI):
                    k, step = c % 2, i - DT_SLOTS[c]
                    n = t.count(4 * KI, 4 * c)
                    x_ps = p_mm[1 - c % 2]
                    if step == 1:
                        act.wait_ge(dt_mm, t.count(KI, c + 1))
                        if t is not OPENING or c > 1:
                            act.wait_ge(sp_dve, t.count(3 * KI, 3 * c - 3))
                            act.wait_ge(du_lo, t.count(2 * KI, 2 * c - 2))
                        act.activation(sp_e[k][:], x_ps[:], ACT.Abs, bias=dtb[:, c:c + 1]).then_inc(sp_act, 1)
                        act.wait_ge(sp_act, n + 1)
                        act.activation(sp_e[k][:], sp_e[k][:], ACT.Exp, scale=-1.0).then_inc(sp_act, 1)
                    elif step == 2:
                        act.wait_ge(sp_act, n + 2)
                        act.activation(sp_w[k][:], sp_e[k][:], ACT.Identity, bias=1.0).then_inc(sp_act, 1)
                        if t is not OPENING or c:
                            act.wait_ge(sp_dve, t.count(3 * KI, 3 * c))
                        act.activation(sp_l[:], sp_e[k][:], ACT.Ln, bias=1.0).then_inc(sp_act, 1)
                    elif step == 3:
                        act.activation(sp_r[k][:], x_ps[:], ACT.Relu, bias=dtb[:, c:c + 1]).then_inc(dt_sb, 1)
                    elif step == 6:
                        act.wait_ge(sp_dve, t.count(3 * KI, 3 * c + 3))
                        split_high(d_parts[par], sp_r[k], c, d_hi)
                    elif step == 8:
                        act.wait_ge(du, t.count(KI, c + 1))
                        split_high(du_parts[par], sp_w[k], c, du_hi)

            def split_high(parts, src, c, done):
                act.activation(parts[0:HALF, 0, c, :], src[0:HALF, :], ACT.Copy).then_inc(done, 1)
                act.activation(parts[HALF:P, 1, c, :], src[HALF:P, :], ACT.Copy).then_inc(done, 1)

            def scan_slot(t, g):
                act.wait_ge(d_bc, t.count(NG, g + 1))
                chunk, quadrant, step = group_place(g)
                act.activation(p_d[d_bank(g)][:], p_d[d_bank(g)][:], ACT.Exp,
                               scale=a_neg[:, g:g + 1]).then_inc(decay, 1)

            def save(t, q):
                act.wait_ge(scanned, t.count(NG, 4 * q + 4 + 2))
                slot = (4 * q) % HRING
                src = (zeros[:, 0:4] if t.tt == TILES_B - 1 else
                       h[:, slot:slot + 4, NT - 1:NT].rearrange("p a b -> p (a b)"))
                act.activation(state[:, 4 * q:4 * q + 4], src, ACT.Copy).then_inc(saved, 1)

            for i in range(FRONT_SLOTS):
                front(OPENING, i)
            for g in range(GC):
                scan_slot(OPENING, g)
                if g % 4 == 2 and g > 3:
                    save(OPENING, g // 4 - 1)
            with act.Fori(0, BATCH) as b:
                for tt in range(TILES_B):
                    t = SeqTile(b, tt)
                    nxt = t.following()
                    for i in range(NG):
                        now, g = (t, i + GC) if i < NG - GC else (nxt, i + GC - NG)
                        scan_slot(now, g)
                        if g % 4 == 2:
                            save(*((now, g // 4 - 1) if g > 3 else (t, QUADS - 1)))
                        front(nxt, i)

        @block.gpsimd
        def _(pool):
            pool.memset(zeros[:], 0.0).then_inc(zeroed, 1)
            pool.sem_inc(hc_done, HRING)

            def times_c(t, g):
                pool.wait_ge(scanned, t.count(NG, g + 1 + 2))
                if g == 0:
                    pool.wait_ge(rows_sb, t.count(2, 2))
                if g % 4 == 0:
                    pool.wait_ge(folded, t.count(QUADS, g // 4 + 1))
                s = g % HRING
                pool.tensor_tensor(hc[:, s, :], h[:, s, :], c_rows[t.tt % 2][:], ALU.mult).then_inc(hc_done, 1)

            def front(t, i):
                for c in range(KI):
                    if i == DT_SLOTS[c] + 6:
                        k = c % 2
                        pool.wait_ge(sp_dve, t.count(3 * KI, 3 * c + 3))
                        pool.wait_ge(silu, t.count(1, 1))
                        pool.tensor_tensor(sp_w[k][:], sp_r[k][:], uz[t.tt % 2][:, c, :],
                                           ALU.mult).then_inc(du, 1)

            def gate(t, c):
                pool.wait_ge(y_sb, t.count(KI, c + 1 + 1))
                zs = uz[t.tt % 2]
                pool.tensor_tensor(zs[:, KI + c, :], zs[:, c, :], zs[:, KI + c, :], ALU.mult).then_inc(gated, 1)

            for i in range(FRONT_SLOTS):
                front(OPENING, i)
            for g in range(1, GC):
                times_c(OPENING, g - 1)
            with pool.Fori(0, BATCH) as b:
                for tt in range(TILES_B):
                    t = SeqTile(b, tt)
                    nxt = t.following()
                    for i in range(NG):
                        times_c(*((t, i + GC - 1) if i <= NG - GC else (nxt, i + GC - 1 - NG)))
                        front(nxt, i)
                        if i % GC == 7:
                            gate(t, i // GC)
            times_c(PAST, GC - 1)

        @block.vector
        def _(dve):
            dve.wait_ge(weights_in, 16 * WEIGHTS)
            ident_sb = uz[1][:, 2, 0:P]
            dve.tensor_copy(pick_r[:], uz[1][:, 0:2, :].rearrange("p a (g m) -> p (a g) m", m=P))
            dve.tensor_copy(spread_bc[:], uz[1][:, 2, P:3 * P].rearrange("p (a m) -> p a m", m=P))
            for j in range(KI):
                for k in range(TAPS):
                    last = dve.tensor_scalar(w_conv[:, j, k, :], ident_sb, taps[:, j, k:k + 1], None, ALU.mult)
            last.then_inc(consts, 1)
            dve.wait_ge(a_exp, 1)
            dve.tensor_scalar(a_neg[:], a_neg[:], -1.0, None, ALU.mult).then_inc(consts, 1)
            dve.sem_inc(scanned, 2)
            dve.sem_inc(dub, 2)
            dve.sem_inc(y_sb, 1)
            dve.sem_inc(out_sb, 1)
            dve.sem_inc(x1_out, 16)

            def times_b(t, g):
                dve.wait_ge(du_bc, t.count(NG, g + 1))
                if g == 0:
                    dve.wait_ge(rows_sb, t.count(2, 2))
                dve.wait_ge(scanned, t.count(NG, g + 1))
                dve.tensor_tensor(db[g % 2][:], p_du[g % 2][:], b_rows[t.tt % 2][:], ALU.mult).then_inc(dub, 1)

            def scan(t, g):
                dve.wait_ge(decay, t.count(NG, g + 1))
                dve.wait_ge(dub, t.count(NG, g + 1 + 2))
                if g % 4 == 0:
                    dve.wait_ge(saved, t.count(QUADS, g // 4 + QUADS - 1))
                dve.wait_ge(hc_done, t.count(NG, g + 1))
                dve.tensor_tensor_scan(h[:, g % HRING, :], p_d[d_bank(g)][:], db[g % 2][:], state[:, g:g + 1],
                                       ALU.mult, ALU.add).then_inc(scanned, 1)

            def front(t, i):
                par = t.tt % 2
                for c in range(KI):
                    k, step = c % 2, i - DT_SLOTS[c]
                    n = t.count(3 * KI, 3 * c)
                    if step == 3:
                        dve.wait_ge(sp_act, t.count(4 * KI, 4 * c + 4))
                        dve.scalar_tensor_tensor(out=sp_w[k][:], in0=sp_w[k][:], scalar=-1.0, in1=sp_l[:],
                                                 op0=ALU.add, op1=ALU.subtract).then_inc(sp_dve, 1)
                    elif step == 4:
                        dve.wait_ge(sp_dve, n + 1)
                        dve.scalar_tensor_tensor(out=sp_e[k][:], in0=sp_w[k][:], scalar=0.0, in1=sp_e[k][:],
                                                 op0=ALU.max, op1=ALU.subtract).then_inc(sp_dve, 1)
                    elif step == 5:
                        dve.wait_ge(sp_dve, n + 2)
                        dve.wait_ge(dt_sb, t.count(KI, c + 1))
                        dve.tensor_tensor(sp_r[k][:], sp_r[k][:], sp_e[k][:], ALU.subtract).then_inc(sp_dve, 1)
                    elif step == 7:
                        dve.wait_ge(d_hi, t.count(2 * KI, 2 * c + 2))
                        split_low(d_parts[par], sp_r[k], c, d_lo)
                    elif step == 9:
                        dve.wait_ge(du_hi, t.count(2 * KI, 2 * c + 2))
                        split_low(du_parts[par], sp_w[k], c, du_lo)

            def split_low(parts, src, c, done):
                dve.tensor_tensor(parts[HALF:P, 0, c, :], src[0:HALF, :],
                                  parts[0:HALF, 0, c, :].bitcast(F32), ALU.subtract).then_inc(done, 1)
                dve.tensor_tensor(parts[0:HALF, 1, c, :], src[HALF:P, :],
                                  parts[HALF:P, 1, c, :].bitcast(F32), ALU.subtract).then_inc(done, 1)

            def skip(t, c):
                u = uz[t.tt % 2][:, c, :]
                dve.wait_ge(folded, t.count(QUADS, 4 * c + 4 + 2))
                dve.scalar_tensor_tensor(out=u, in0=u, scalar=dpar[:, c:c + 1], in1=p_y[:],
                                         op0=ALU.mult, op1=ALU.add).then_inc(y_sb, 1)

            def residual(t, s):
                dve.wait_ge(out_mm, t.count(SUB, s + 1))
                if s == 0:
                    dve.wait_ge(x_in, t.count(16, 16))
                dve.tensor_tensor(res[:, s, :], p_mm[s % 2][:, 0:DM], x_nat[:, s, :], ALU.add).then_inc(out_sb, 1)

            N_LN = 1 + 3 + 16

            def norm(t):
                count = [0]

                def link(ins):
                    count[0] += 1
                    ins.then_inc(ln_dve, 1)
                    dve.wait_ge(ln_dve, t.count(SUB * 2 + N_LN, count[0]))

                dve.wait_ge(out_sb, t.count(SUB, SUB + 1))
                for s in range(SUB):
                    last = dve.bn_stats(stats[:, s, :], res[:, s, :])
                    last.then_inc(ln_dve, 1)
                dve.wait_ge(ln_dve, t.count(SUB * 2 + N_LN, SUB))
                dve.sem_inc(waited, 1)
                for s in range(SUB):
                    dve.bn_aggr(mv[:, s, :], stats[:, s, :]).then_inc(ln_dve, 1)
                count[0] = 2 * SUB
                dve.wait_ge(ln_dve, t.count(SUB * 2 + N_LN, 2 * SUB))
                link(dve.tensor_copy(var4[:], mv[:, :, 1:2].rearrange("p a b -> p (a b)")))
                rstd_newton(dve, link, var4, y4, a4)
                for s in range(SUB):
                    dve.tensor_scalar(res[:, s, :], res[:, s, :], mv[:, s, 0:1], y4[:, s:s + 1],
                                      ALU.subtract, ALU.mult).then_inc(ln_out, 1)

            for i in range(FRONT_SLOTS):
                front(OPENING, i)
            for g in range(GC):
                times_b(OPENING, g)
                if g:
                    scan(OPENING, g - 1)
            with dve.Fori(0, BATCH) as b:
                for tt in range(TILES_B):
                    t = SeqTile(b, tt)
                    nxt = t.following()
                    for i in range(NG):
                        now, g = (t, i + GC) if i < NG - GC else (nxt, i + GC - NG)
                        times_b(now, g)
                        scan(*((now, g - 1) if g else (t, NG - 1)))
                        front(nxt, i)
                        if i % GC == 6:
                            skip(t, i // GC)
                        if 59 <= i < 63:
                            if i == 59:
                                dve.wait_ge(x1_out, t.count(16, 16))
                            residual(t, i - 59)
                        if i == 63:
                            norm(t)
            scan(PAST, GC - 1)


W_COLS = (2 * KM + 2 * KH) * DH + KH * DM
W1_AT, W2_AT, H1_AT, H2_AT, W3_AT = 0, KM * DH, 2 * KM * DH, (2 * KM + KH) * DH, (2 * KM + 2 * KH) * DH


def ffn_stage(nc, sems, ctx, split, branch, weights, x1, scales, s3, ident, out):
    tag = "s_" if split else "g_"
    WT = F32R if split else F32
    parts = 2 if split else 1

    def sb(name, shape, dt=F32):
        return ctx.enter_context(nc.sbuf_tensor(tag + name, shape, dt))

    def sem(name):
        return sems.enter_context(nc.semaphore(tag + name))

    x_nat = [sb(f"x_nat{i}", [P, SUB, DM]) for i in range(2)]
    x_t = [[sb(f"x_t{i}{j}", [P, KM, NT], WT) for j in range(parts)] for i in range(2)]
    acts = [[sb(f"act{i}{j}", [P, KH, NT], WT) for j in range(parts)] for i in range(2)]
    hring = [sb(f"h{i}", [P, NT]) for i in range(3)] if split else None
    silu_t = [sb(f"silu{i}", [P, NT]) for i in range(2)]
    res = sb("res", [P, SUB, DM])
    sc = sb("sc", [P, 4, KH])
    s3b = sb("s3b", [P, DM])
    idn = sb("idn", [P, P])
    stats = sb("stats", [P, SUB, 6])
    mv = sb("mv", [P, SUB, 2])
    var4, y4, a4 = sb("var4", [P, SUB]), sb("y4", [P, SUB]), sb("a4", [P, SUB])
    bank = [ctx.enter_context(nc.psum_tensor(f"{tag}bank{i}", [P, NT], F32)) for i in range(8)]
    p_w1, p_w2, p_h, p_o = bank[0:2], bank[2:4], bank[4:6], bank[6:8]

    consts_in, stored = sem("consts_in"), sem("stored")
    x_in = [sem("x_in0"), sem("x_in1")]
    tr_mm, w1_mm, w2_mm, h_mm, o_mm = (sem(s) for s in ("tr_mm", "w1_mm", "w2_mm", "h_mm", "o_mm"))
    xt_hi, xt_lo = sem("xt_hi"), sem("xt_lo")
    silu, gate, gelu = sem("silu"), sem("gate"), sem("gelu")
    hi, lo = sem("hi"), sem("lo")
    scaled, summed = sem("scaled"), sem("summed")
    ln_dve, ln_out = sem("ln_dve"), sem("ln_out")
    waited = sem("waited")
    STEPS = TILES // PairTile.OF_STEP
    first = PairTile(0, 0)
    L3 = 3 * KH

    block = ctx.enter_context(nc.Block())

    @block.sync
    def _(sp):
        def body():
            for k in range(4):
                sp.dma_start(sc[:, k, :], scales[k]).then_inc(consts_in, 16)
            sp.dma_start(s3b[:], s3).then_inc(consts_in, 16)
            sp.dma_start(idn[:], ident).then_inc(consts_in, 16)

            def load(t):
                row = t.b * (2 * NT) + t.tt * NT
                if t is not first:
                    row = row % (BATCH * SEQ)
                sp.dma_start(x_nat[t.tt][:], x1[bass.ds(row, NT), :].rearrange("(s p) c -> p s c", p=P))\
                  .then_inc(x_in[t.tt], 16)

            load(first)
            with sp.Fori(0, STEPS) as b:
                for tt in range(2):
                    t = PairTile(b, tt)
                    sp.wait_ge(summed, t.count(SUB, SUB))
                    sp.sem_inc(waited, 1)
                    load(t.following())
                    sp.wait_ge(ln_out, t.count(SUB, SUB))
                    sp.sem_inc(waited, 1)
                    sp.dma_start(out[bass.ds(b * (2 * NT) + tt * NT, NT), :]
                                 .rearrange("(s p) c -> p s c", p=P), res[:]).then_inc(stored, 16)
            sp.wait_ge(stored, 16 * TILES + 16)
        branch(sp, body)

    @block.tensor
    def _(pe):
        def body():
            pe.wait_ge(consts_in, 16 * 6)

            def product(dst, n_k, w_at, ins, rows_w, cols, wait=None):
                for k in range(n_k):
                    if wait:
                        wait(k)
                    for j in range(parts):
                        last = pe.matmul(dst, weights[:, w_at + k * rows_w + cols:w_at + k * rows_w + cols + P],
                                         ins[j][:, k, :], start=k == 0 and j == 0,
                                         stop=k == n_k - 1 and j == parts - 1)
                return last

            def transposes(t):
                pe.wait_ge(x_in[t.tt], t.b * 16 + 16)
                for k in range(KM):
                    if t is not first:
                        pe.wait_ge(scaled, PairTile(t.b, t.tt - 1).count(SUB, SUB))
                    for s in range(SUB):
                        last = pe.transpose(p_o[k][:, s * P:(s + 1) * P], x_nat[t.tt][:, s, k * P:(k + 1) * P],
                                            idn[:])
                    last.then_inc(tr_mm, 1)

            def gated(t):
                pe.wait_ge(xt_lo if split else xt_hi, t.count(KM, KM))
                for m in range(KH):
                    pe.wait_ge(silu, t.count(KH, m + 1))
                    product(p_w1[m % 2][:], KM, W1_AT, x_t[t.tt], DH, m * P).then_inc(w1_mm, 1)
                    pe.wait_ge(gate, t.count(KH, m + 1))
                    product(p_w2[m % 2][:], KM, W2_AT, x_t[t.tt], DH, m * P).then_inc(w2_mm, 1)

            def hidden(t, layer):
                w_at = (H1_AT, H2_AT)[layer]
                done = lo if split else (gate, gelu)[layer]

                def arrived(k):
                    if split:
                        pe.wait_ge(lo, t.count(L3, layer * KH + k + 1))
                    elif layer == 0:
                        pe.wait_ge(gate, t.count(KH, k + 1 + 2))
                    else:
                        pe.wait_ge(gelu, t.count(2 * KH, k + 1 + 2))
                for m in range(KH):
                    pe.wait_ge(gelu, t.count(2 * KH, layer * KH + m + 1))
                    product(p_h[m % 2][:], KH, w_at, acts[layer], DH, m * P,
                            arrived if m == 0 else None).then_inc(h_mm, 1)
                    if layer == 1 and m == 3:
                        transposes(t.following())

            def output(t):
                for s in range(SUB):
                    if s < 2:
                        nxt = t.following()
                        pe.wait_ge(xt_lo if split else xt_hi, nxt.count(KM, s + 1))
                    else:
                        pe.wait_ge(scaled, t.count(SUB, s - 1 + 4))
                    for k in range(KH):
                        if s == 0:
                            if split:
                                pe.wait_ge(lo, t.count(L3, 2 * KH + k + 1))
                            else:
                                pe.wait_ge(gelu, t.count(2 * KH, KH + k + 1 + 2))
                        for j in range(parts):
                            last = pe.matmul(p_o[s % 2][:, 0:DM], acts[0][j][:, k, s * P:(s + 1) * P],
                                             weights[:, W3_AT + k * DM:W3_AT + (k + 1) * DM],
                                             start=k == 0 and j == 0, stop=k == KH - 1 and j == parts - 1)
                    last.then_inc(o_mm, 1)

            transposes(first)
            gated(first)
            with pe.Fori(0, STEPS) as b:
                for tt in range(2):
                    t = PairTile(b, tt)
                    hidden(t, 0)
                    hidden(t, 1)
                    output(t)
                    gated(t.following())
        branch(pe, body)

    @block.scalar
    def _(act):
        def body():
            act.wait_ge(consts_in, 16 * 6)
            act.sem_inc(silu, 2)
            act.sem_inc(gelu, 2)

            def transposed(t):
                for k in range(KM):
                    act.wait_ge(tr_mm, t.count(KM, k + 1))
                    act.activation(x_t[t.tt][0][:, k, :], p_o[k][:], ACT.Copy).then_inc(xt_hi, 1)

            def high(t, c):
                if c < KH:
                    act.wait_ge(gate, t.count(KH, c + 1 + 2))
                else:
                    act.wait_ge(gelu, t.count(2 * KH, c - KH + 1 + 2))
                act.activation(acts[(c // KH) % 2][0][:, c % KH, :], hring[c % 3][:], ACT.Copy).then_inc(hi, 1)

            def gated(t):
                for m in range(KH):
                    act.wait_ge(w1_mm, t.count(KH, m + 1))
                    if m > 1 or t is not first:
                        act.wait_ge(gate, t.count(KH, m - 2 + 1 + 2))
                    act.activation(silu_t[m % 2][:], p_w1[m % 2][:], ACT.Silu,
                                   scale=sc[:, 0, m:m + 1]).then_inc(silu, 1)
                    if split and m:
                        high(t, m - 1)
                if split:
                    high(t, KH - 1)

            def hidden(t, layer):
                for m in range(KH):
                    c = (layer + 1) * KH + m
                    act.wait_ge(h_mm, t.count(2 * KH, layer * KH + m + 1))
                    if split:
                        act.wait_ge(lo, t.count(L3, c - 2))
                        dst = hring[c % 3][:]
                    else:
                        dst = acts[1 - layer][0][:, m, :]
                    act.activation(dst, p_h[m % 2][:], ACT.Gelu,
                                   scale=sc[:, 2 + layer, m:m + 1]).then_inc(gelu, 1)
                    if split:
                        high(t, c)
                    if layer == 1 and m == 4:
                        transposed(t.following())

            transposed(first)
            gated(first)
            with act.Fori(0, STEPS) as b:
                for tt in range(2):
                    t = PairTile(b, tt)
                    hidden(t, 0)
                    hidden(t, 1)
                    gated(t.following())
        branch(act, body)

    @block.vector
    def _(dve):
        def body():
            dve.wait_ge(consts_in, 16 * 6)
            dve.sem_inc(gate, 2)
            dve.sem_inc(scaled, 4)
            dve.sem_inc(summed, 4)
            dve.sem_inc(stored, 16)

            def transposed(t):
                if split:
                    for k in range(KM):
                        dve.wait_ge(xt_hi, t.count(KM, k + 1))
                        dve.tensor_tensor(x_t[t.tt][1][:, k, :], p_o[k][:], x_t[t.tt][0][:, k, :].bitcast(F32),
                                          ALU.subtract).then_inc(xt_lo, 1)

            def low(t, c):
                a = acts[(c // KH) % 2]
                dve.wait_ge(hi, t.count(L3, c + 1))
                dve.tensor_tensor(a[1][:, c % KH, :], hring[c % 3][:], a[0][:, c % KH, :].bitcast(F32),
                                  ALU.subtract).then_inc(lo, 1)

            def gated(t):
                for m in range(KH):
                    dve.wait_ge(w2_mm, t.count(KH, m + 1))
                    dve.wait_ge(silu, t.count(KH, m + 1 + 2))
                    if split and (m > 2 or t is not first):
                        dve.wait_ge(lo, t.count(L3, m - 2))
                    dst = hring[m % 3][:] if split else acts[0][0][:, m, :]
                    dve.scalar_tensor_tensor(out=dst, in0=p_w2[m % 2][:], scalar=sc[:, 1, m:m + 1],
                                             in1=silu_t[m % 2][:], op0=ALU.mult, op1=ALU.mult).then_inc(gate, 1)
                    if split and m:
                        low(t, m - 1)
                if split:
                    low(t, KH - 1)

            def hidden(t, layer):
                for m in range(KH):
                    if split:
                        low(t, (layer + 1) * KH + m)
                    if layer == 1 and m == 4:
                        transposed(t.following())

            def residual(t):
                for s in range(SUB):
                    dve.wait_ge(o_mm, t.count(SUB, s + 1))
                    if s == 0:
                        dve.wait_ge(stored, t.count(16, 16))
                    dve.tensor_tensor(res[:, s, :], p_o[s % 2][:, 0:DM], s3b[:], ALU.mult).then_inc(scaled, 1)
                    dve.wait_ge(scaled, t.count(SUB, s + 1 + 4))
                    dve.tensor_tensor(res[:, s, :], res[:, s, :], x_nat[t.tt][:, s, :], ALU.add).then_inc(summed, 1)

            N_LN = 2 * SUB + 1 + 3 + 16

            def norm(t):
                count = [2 * SUB]

                def link(ins):
                    count[0] += 1
                    ins.then_inc(ln_dve, 1)
                    dve.wait_ge(ln_dve, t.count(N_LN, count[0]))

                dve.wait_ge(summed, t.count(SUB, SUB + 4))
                for s in range(SUB):
                    dve.bn_stats(stats[:, s, :], res[:, s, :]).then_inc(ln_dve, 1)
                dve.wait_ge(ln_dve, t.count(N_LN, SUB))
                dve.sem_inc(waited, 1)
                for s in range(SUB):
                    dve.bn_aggr(mv[:, s, :], stats[:, s, :]).then_inc(ln_dve, 1)
                dve.wait_ge(ln_dve, t.count(N_LN, 2 * SUB))
                link(dve.tensor_copy(var4[:], mv[:, :, 1:2].rearrange("p a b -> p (a b)")))
                rstd_newton(dve, link, var4, y4, a4)
                for s in range(SUB):
                    dve.tensor_scalar(res[:, s, :], res[:, s, :], mv[:, s, 0:1], y4[:, s:s + 1],
                                      ALU.subtract, ALU.mult).then_inc(ln_out, 1)

            transposed(first)
            gated(first)
            with dve.Fori(0, STEPS) as b:
                for tt in range(2):
                    t = PairTile(b, tt)
                    hidden(t, 0)
                    hidden(t, 1)
                    residual(t)
                    gated(t.following())
                    norm(t)
        branch(dve, body)


def weight_pieces(a):
    for name in ("w1T", "w2T", "h1T", "h2T", "w3T"):
        w = a[name]
        for k in range(w.shape[0] // P):
            yield w[k * P:(k + 1) * P, :]


def round_weights(nc, sems, ctx, a, flag):
    pieces = list(weight_pieces(a))
    n, ring = len(pieces), 4
    cols = [piece.shape[1] for piece in pieces]
    at = [sum(cols[:i]) for i in range(n)]
    weights = ctx.enter_context(nc.sbuf_tensor("weights_r", [P, W_COLS], F32R))
    with ExitStack() as own:
        stage = [own.enter_context(nc.sbuf_tensor(f"stage{i}", [P, DH], F32)) for i in range(ring)]
        lost = [own.enter_context(nc.sbuf_tensor(f"lost{i}", [P, DH], F32)) for i in range(2)]
        worst = own.enter_context(nc.sbuf_tensor("worst", [P, n], F32))
        top = own.enter_context(nc.sbuf_tensor("top", [P, 1], F32))
        exact = own.enter_context(nc.sbuf_tensor("exact", [P, 1], F32))
        ones = own.enter_context(nc.sbuf_tensor("ones", [P, 1], F32))
        total = own.enter_context(nc.psum_tensor("total", [P, 1], F32))
        loaded = [sems.enter_context(nc.semaphore(f"w_loaded{i}")) for i in range(ring)]
        rounded, measured, took, counted, checked, flag_out = (
            sems.enter_context(nc.semaphore(s)) for s in
            ("w_rounded", "w_measured", "w_took", "w_counted", "w_checked", "flag_out"))
        with nc.Block() as block:
            @block.sync
            def _(sp):
                for i, piece in enumerate(pieces):
                    if i >= ring:
                        sp.wait_ge(took, i - ring + 1)
                    sp.dma_start(stage[i % ring][:, 0:cols[i]], piece).then_inc(loaded[i % ring], 16)

            @block.scalar
            def _(act):
                for i in range(n):
                    act.wait_ge(loaded[i % ring], 16 * (i // ring + 1))
                    act.activation(weights[:, at[i]:at[i] + cols[i]], stage[i % ring][:, 0:cols[i]],
                                   ACT.Copy).then_inc(rounded, 1)

            @block.vector
            def _(dve):
                dve.memset(ones[:], 1.0)
                for i in range(n + 1):
                    if i < n:
                        dve.wait_ge(rounded, i + 1)
                        if i >= 2:
                            dve.wait_ge(measured, i - 1)
                        dve.tensor_tensor(lost[i % 2][:, 0:cols[i]], stage[i % ring][:, 0:cols[i]],
                                          weights[:, at[i]:at[i] + cols[i]].bitcast(F32),
                                          ALU.not_equal).then_inc(took, 1)
                    if i:
                        dve.wait_ge(took, i)
                        dve.tensor_reduce(worst[:, i - 1:i], lost[(i - 1) % 2][:, 0:cols[i - 1]],
                                          mybir.AxisListType.X, ALU.max).then_inc(measured, 1)
                dve.wait_ge(measured, n)
                dve.tensor_reduce(top[:], worst[:], mybir.AxisListType.X, ALU.max).then_inc(measured, 1)
                dve.wait_ge(measured, n + 1)
                dve.tensor_scalar(exact[:], top[:], 0.0, None, ALU.is_equal).then_inc(measured, 1)
                dve.wait_ge(counted, 1)
                dve.tensor_scalar(flag[0:1, 0:1], total[0:1, :], float(P), None,
                                  ALU.is_equal).then_inc(checked, 1)

            @block.tensor
            def _(pe):
                pe.wait_ge(measured, n + 2)
                pe.matmul(total[0:1, :], ones[:], exact[:], start=True, stop=True).then_inc(counted, 1)
    return weights


def load_float32_weights(nc, sems, ctx, a, branch):
    weights = ctx.enter_context(nc.sbuf_tensor("weights_f32", [P, W_COLS], F32))
    loaded = sems.enter_context(nc.semaphore("weights_f32_in"))
    with nc.Block() as block:
        @block.sync
        def _(sp):
            def body():
                at = n = 0
                for piece in weight_pieces(a):
                    sp.dma_start(weights[:, at:at + piece.shape[1]], piece).then_inc(loaded, 16)
                    at += piece.shape[1]
                    n += 1
                sp.wait_ge(loaded, 16 * n)
            branch(sp, body)
    return weights


def program(nc, a, x1, out):
    with ExitStack() as sems:
        mamba_stage(nc, sems, a["xT"], a["x"], a["in_wT"], a["conv_w"], a["conv_b"], a["xp_wT"], a["dt_wT"],
                    a["dt_b"], a["A_log"], a["D_param"], a["out_wT"], a["pick"], a["fold"], a["ident"], x1)
        x1_rows, out_rows = (v.rearrange("b l c -> (b l) c") for v in (x1, out))
        scales = [a["s1"], a["s2"], a["sh1"], a["sh2"]]
        ident = a["ident"][:, 0:1, :].rearrange("p a m -> p (a m)")
        flag = sems.enter_context(nc.sbuf_tensor("flag", [P, 1], I32))

        def when(value):
            def branch(eng, body):
                exact = eng.value_load(flag[0:1, 0:1], min_val=0, max_val=1)
                with eng.If(exact == value):
                    body()
            return branch

        with ExitStack() as ctx:
            weights = round_weights(nc, sems, ctx, a, flag)
            ffn_stage(nc, sems, ctx, True, when(1), weights, x1_rows, scales, a["s3"], ident, out_rows)
        with ExitStack() as ctx:
            weights = load_float32_weights(nc, sems, ctx, a, when(0))
            ffn_stage(nc, sems, ctx, False, when(0), weights, x1_rows, scales, a["s3"], ident, out_rows)


def shape_constants():
    pick = np.zeros((P, HALF // GD, P), np.float32)
    fold = np.zeros((P, 4, 32), np.float32)
    ident = np.zeros((P, 3, P), np.float32)
    ident[:, 0] = np.eye(P)
    for d in range(GD):
        for n in range(NS):
            row = d * NS + n
            for which in range(HALF // GD):
                pick[which * GD + d, which, row] = 1
                pick[HALF + which * GD + d, which, row] = 1
            for step in range(4):
                fold[row, step, step * GD + d] = 1
            ident[DTR + n, 1, row] = 1
            ident[DTR + NS + n, 2, row] = 1
    return pick, fold, ident


def kernel(**inputs):
    import concourse.bacc as bacc
    from concourse.bass_utils import run_bass_kernel_spmd

    v = {k.removeprefix("L0_"): np.asarray(x) for k, x in inputs.items()}
    pick, fold, ident = shape_constants()

    def column(x):
        return np.ascontiguousarray(x.reshape(-1, P).T)

    a_log = v["attn_A_log"].reshape(KI, 4, 4, GD, NS).transpose(3, 4, 0, 2, 1).reshape(P, NG)
    arrays = {
        "x": v["attn_hidden_states"],
        "xT": v["attn_hidden_states"].transpose(0, 2, 1),
        "in_wT": v["attn_in_proj_w"].T, "conv_w": v["attn_conv_w"], "conv_b": column(v["attn_conv_b"]),
        "xp_wT": v["attn_x_proj_w"].T, "dt_wT": v["attn_dt_proj_w"].T, "dt_b": column(v["attn_dt_proj_b"]),
        "A_log": a_log, "D_param": column(v["attn_D_param"]), "out_wT": v["attn_out_proj_w"].T,
        "pick": pick, "fold": fold, "ident": ident,
        "w1T": v["ffn_w1_w"].T, "w2T": v["ffn_w2_w"].T, "h1T": v["ffn_h1_w"].T, "h2T": v["ffn_h2_w"].T,
        "w3T": v["ffn_w3_w"].T,
        "s1": column(v["ffn_w1_s"]), "s2": column(v["ffn_w2_s"]), "sh1": column(v["ffn_h1_s"]),
        "sh2": column(v["ffn_h2_s"]), "s3": np.broadcast_to(v["ffn_w3_s"], (P, DM)),
    }
    arrays = {k: np.ascontiguousarray(x) for k, x in arrays.items()}
    nc = bacc.Bacc("TRN2", target_bir_lowering=False, num_devices=1)
    aps = {k: nc.dram_tensor(f"in_{k}", x.shape, mybir.dt.from_np(x.dtype), kind="ExternalInput").ap()
           for k, x in arrays.items()}
    x1 = nc.dram_tensor("x1", (BATCH, SEQ, DM), F32, kind="Internal").ap()
    out = nc.dram_tensor("out", (BATCH, SEQ, DM), F32, kind="ExternalOutput").ap()
    program(nc, aps, x1, out)
    r = run_bass_kernel_spmd(nc, [{f"in_{k}": x for k, x in arrays.items()}], core_ids=[0])
    return r.results[0]["out"]
```

```python
import concourse.bass as bass
from concourse import mybir
from contextlib import ExitStack
import numpy as np

F32 = mybir.dt.float32
F32R = mybir.dt.float32r
I32 = mybir.dt.int32
ALU = mybir.AluOpType
ACT = mybir.ActivationFunctionType

P = 128
BATCH, SEQ, DM = 4, 2048, 256
DI, NS, DTR, TAPS = 512, 16, 64, 4
DH = 1024
NT = 512
TILES_B = SEQ // NT
TILES = BATCH * TILES_B
KM, KI, KH = DM // P, DI // P, DH // P
SUB = NT // P
GD = P // NS
NG = DI // GD
GC = P // GD
QUADS = NG // 4
HALF = P // 2
HRING = 8
EPS = 1e-5
EXP_LN = "natural_log_exp_and_others"
RSQRT_SEED = float(0x5F3759DF)


def group_place(g):
    chunk, k = divmod(g, GC)
    quadrant, step = k % 4, k // 4
    return chunk, quadrant, step


class Tile:

    def __init__(self, b, tt):
        self.b, self.tt = b, tt

    def count(self, per_tile, n):
        return self.b * (self.OF_STEP * per_tile) + (self.tt * per_tile + n)

    def following(self):
        if self.tt + 1 < self.OF_STEP:
            return type(self)(self.b, self.tt + 1)
        return type(self)(self.b + 1, 0)


class SeqTile(Tile):
    OF_STEP = TILES_B


class PairTile(Tile):
    OF_STEP = 2


CONV_SLOTS = [i for i in range(KI * (TAPS + 1)) if i % (TAPS + 1) > 0]
SILU_U_SLOT = CONV_SLOTS[-1] + 1
XD_SLOTS = range(27, 27 + KI)
ROWS_SLOTS, DT_SLOTS = (XD_SLOTS.stop + 1, XD_SLOTS.stop + 3), (33, 38, 43, 48)
BETWEEN = [i for i in range(DT_SLOTS[0] + 4, NG) if i not in DT_SLOTS]
Z_SLOTS, X_SLOTS = BETWEEN[:KI * KM], BETWEEN[KI * KM:2 * KI * KM]
SILU_Z_SLOT = 58
FRONT_SLOTS = DT_SLOTS[-1] + 11
OUT_SLOTS = {57: ((0, 0, 2),), 58: ((1, 0, 2),), 59: ((0, 3, 3), (1, 3, 3)), 61: ((2, 0, 3),), 62: ((3, 0, 3),)}
SUM_SLOTS = (59, 60, 62, 63)
LEAD = 4
HOLD = {SILU_U_SLOT: 3, SILU_Z_SLOT: 2}
DRING, DBRING = 8, 4


def at_group(t, n):
    return (t, n) if n < NG else (t.following(), n - NG)


def decays_of_slot(i):
    for silu, hold in HOLD.items():
        if silu < i <= silu + hold:
            return ()
        if silu + hold < i <= silu + 2 * hold:
            n = GC + LEAD + silu + 1 + 2 * (i - silu - hold - 1)
            return n, n + 1
    return (GC + LEAD + i,)


OPENING = SeqTile(0, 0)
SECOND = SeqTile(0, 1)
PAST = SeqTile(BATCH, 0)


N_RSTD = 3 + 4 * 4


def rstd_step(dve, n, var4, y4, a4):
    if n == 0:
        return dve.tensor_scalar(var4[:], var4[:], EPS, None, ALU.add)
    if n == 1:
        return dve.tensor_scalar(a4[:].bitcast(I32), var4[:].bitcast(I32), 1, None, ALU.logical_shift_right)
    if n == 2:
        return dve.tensor_scalar(y4[:].bitcast(I32), a4[:].bitcast(I32), -1.0, RSQRT_SEED, ALU.mult, ALU.add)
    if n % 4 == 3:
        return dve.tensor_tensor(a4[:], y4[:], y4[:], ALU.mult)
    if n % 4 == 0:
        return dve.tensor_tensor(a4[:], a4[:], var4[:], ALU.mult)
    if n % 4 == 1:
        return dve.tensor_scalar(a4[:], a4[:], -0.5, 1.5, ALU.mult, ALU.add)
    return dve.tensor_tensor(y4[:], y4[:], a4[:], ALU.mult)


def mamba_stage(nc, sems, xT, x, in_wT, conv_w, conv_b, xp_wT, dt_wT, dt_b, A_log, D_param, out_wT,
                pick, fold, ident, x1):
    ctx = ExitStack()
    with ctx:
        def sb(name, shape, dt=F32):
            return ctx.enter_context(nc.sbuf_tensor(name, shape, dt))

        def sem(name):
            return sems.enter_context(nc.semaphore(name))

        w_in = sb("w_in", [P, KM, 2 * DI])
        w_xp = sb("w_xp", [P, KI, DTR + 2 * NS])
        w_dt = sb("w_dt", [DTR, DI])
        w_out = sb("w_out", [P, KI, DM])
        w_conv = sb("w_conv", [P, KI, TAPS, P])
        pick_r = sb("pick_r", [P, HALF // GD, P], F32R)
        fold_w = sb("fold_w", [P, 4, 32])
        spread_bc = sb("spread_bc", [P, 2, P])
        taps = sb("taps", [P, KI, TAPS])
        cb = sb("cb", [P, KI])
        dtb = sb("dtb", [P, KI])
        dpar = sb("dpar", [P, KI])
        a_neg = sb("a_neg", [P, NG])
        zeros = sb("zeros", [P, NG])
        xT_sb = [sb(f"xT_sb{i}", [P, KM, NT]) for i in range(2)]
        x_nat = sb("x_nat", [P, SUB, DM])
        res = sb("res", [P, SUB, DM])
        xb = sb("xb", [P, KI, TAPS - 1 + NT])
        uz = [sb(f"uz{i}", [P, 2 * KI, NT]) for i in range(2)]
        d_parts = sb("d_parts", [P, 2, KI, NT], F32R)
        du_parts = sb("du_parts", [P, 2, KI, NT], F32R)
        b_rows = [sb(f"b_rows{i}", [P, NT]) for i in range(2)]
        c_rows = [sb(f"c_rows{i}", [P, NT]) for i in range(2)]
        sp_e = [sb(f"sp_e{i}", [P, NT]) for i in range(2)]
        sp_w = [sb(f"sp_w{i}", [P, NT]) for i in range(2)]
        sp_l = sb("sp_l", [P, NT])
        sp_r = [sb(f"sp_r{i}", [P, NT]) for i in range(2)]
        decays = sb("decays", [P, DRING, NT])
        db = sb("db", [P, DBRING, NT])
        h = sb("h", [P, HRING, NT])
        hc = sb("hc", [P, HRING, NT])
        state = sb("state", [P, NG])
        stats = sb("stats", [P, SUB, 6])
        mv = sb("mv", [P, SUB, 2])
        var4 = sb("var4", [P, SUB])
        y4 = sb("y4", [P, SUB])
        a4 = sb("a4", [P, SUB])
        xd = sb("xd", [DTR + 2 * NS, NT])

        bank = [ctx.enter_context(nc.psum_tensor(f"bank{i}", [P, NT], F32)) for i in range(8)]
        p_mm, p_dt, p_d, p_du, p_y = bank[0:2], bank[2], bank[3:5], bank[5:7], bank[7]

        weights_in = sem("weights_in")
        zeroed = sem("zeroed")
        a_exp = sem("a_exp")
        consts = sem("consts")
        xT_in, x_in, x1_out = sem("xT_in"), sem("x_in"), sem("x1_out")
        x_mm, z_mm, conv_mm, xd_mm, rows_mm, dt_mm, out_mm = (
            sem(s) for s in ("x_mm", "z_mm", "conv_mm", "xd_mm", "rows_mm", "dt_mm", "out_mm"))
        x_sb, z_sb, conv_sb, xd_sb, rows_sb, dt_sb, out_sb = (
            sem(s) for s in ("x_sb", "z_sb", "conv_sb", "xd_sb", "rows_sb", "dt_sb", "out_sb"))
        halo, silu_u, silu_z = sem("halo"), sem("silu_u"), sem("silu_z")
        sp_act = sem("sp_act")
        sp_dve = sem("sp_dve")
        delta = sem("delta")
        d_hi, d_lo, du, du_hi, du_lo = (sem(s) for s in ("d_hi", "d_lo", "du", "du_hi", "du_lo"))
        d_bc, du_bc = sem("d_bc"), sem("du_bc")
        decay = sem("decay")
        dub = sem("dub")
        scanned = sem("scanned")
        saved = sem("saved")
        hc_done = sem("hc_done")
        folded = sem("folded")
        y_sb, gated = sem("y_sb"), sem("gated")
        ln_dve, ln_out = sem("ln_dve"), sem("ln_out")
        waited = sem("waited")

        block = ctx.enter_context(nc.Block())

        WEIGHTS = 12

        @block.sync
        def _(sp):
            for dst, src in (
                (w_in[:], in_wT.rearrange("(k p) e -> p k e", p=P)),
                (w_xp[:], xp_wT.rearrange("(k p) e -> p k e", p=P)),
                (w_dt[:], dt_wT),
                (w_out[:], out_wT.rearrange("(k p) e -> p k e", p=P)),
                (taps[:], conv_w.rearrange("(k p) w -> p k w", p=P)),
                (cb[:], conv_b),
                (dtb[:], dt_b),
                (dpar[:], D_param),
                (a_neg[:], A_log),
                (fold_w[:], fold),
                (uz[1][:, 0:2, :].rearrange("p a (g m) -> p (a g) m", m=P), pick),
                (uz[1][:, 2, 0:3 * P].rearrange("p (a m) -> p a m", m=P), ident),
            ):
                sp.dma_start(dst, src).then_inc(weights_in, 16)

            def load_xT(t):
                row = t.b if isinstance(t.b, int) else t.b % BATCH
                sp.dma_start(xT_sb[t.tt % 2][:], xT[row, :, t.tt * NT:(t.tt + 1) * NT]
                             .rearrange("(k p) t -> p k t", p=P)).then_inc(xT_in, 16)

            load_xT(OPENING)
            sp.wait_ge(x_mm, KI)
            load_xT(SECOND)
            with sp.Fori(0, BATCH) as b:
                for tt in range(TILES_B):
                    t = SeqTile(b, tt)
                    nxt = t.following()
                    sp.wait_ge(z_mm, t.count(KI, KI))
                    sp.sem_inc(waited, 1)
                    sp.wait_ge(x_mm, nxt.count(KI, KI))
                    sp.sem_inc(waited, 1)
                    load_xT(nxt.following())
                    sp.wait_ge(out_sb, t.count(SUB, 1))
                    sp.sem_inc(waited, 1)
                    sp.dma_start(x_nat[:], x[b, tt * NT:(tt + 1) * NT, :]
                                 .rearrange("(s p) c -> p s c", p=P)).then_inc(x_in, 16)
                    sp.wait_ge(ln_out, t.count(SUB, 2 * SUB))
                    sp.sem_inc(waited, 1)
                    sp.dma_start(x1[b, tt * NT:(tt + 1) * NT, :]
                                 .rearrange("(s p) c -> p s c", p=P), res[:]).then_inc(x1_out, 16)
            sp.wait_ge(x1_out, 16 * TILES + 16)

        @block.tensor
        def _(pe):
            pe.wait_ge(weights_in, 16 * WEIGHTS)
            pe.wait_ge(consts, 2)
            pe.sem_inc(folded, 2)

            def x_product(t, j, k):
                if k == 0:
                    if j == 0:
                        pe.wait_ge(xT_in, t.count(16, 16))
                    if j >= 2:
                        pe.wait_ge(x_sb, t.count(KI, j - 1))
                    elif t is not OPENING:
                        pe.wait_ge(z_sb, SeqTile(t.b, t.tt - 1).count(KI, j + 3))
                last = pe.matmul(p_mm[j % 2][:], w_in[:, k, j * P:(j + 1) * P], xT_sb[t.tt % 2][:, k, :],
                                 start=k == 0, stop=k == KM - 1)
                if k == KM - 1:
                    last.then_inc(x_mm, 1)

            def z_product(t, j, k):
                if k == 0:
                    if j >= 2:
                        pe.wait_ge(z_sb, t.count(KI, j - 1))
                    else:
                        pe.wait_ge(rows_sb, t.count(2, 2))
                last = pe.matmul(p_mm[j % 2][:], w_in[:, k, DI + j * P:DI + (j + 1) * P], xT_sb[t.tt % 2][:, k, :],
                                 start=k == 0, stop=k == KM - 1)
                if k == KM - 1:
                    last.then_inc(z_mm, 1)

            def conv_product(t, j, k):
                if k == 0:
                    if j == 0:
                        pe.wait_ge(x_sb, t.count(KI, KI))
                    if j >= 2:
                        pe.wait_ge(conv_sb, t.count(KI, j - 1))
                    elif t is not OPENING:
                        pe.wait_ge(out_sb, SeqTile(t.b, t.tt - 1).count(SUB, 1))
                last = pe.matmul(p_mm[j % 2][:], w_conv[:, j, k, :], xb[:, j, k:k + NT],
                                 start=k == 0, stop=k == TAPS - 1)
                if k == TAPS - 1:
                    last.then_inc(conv_mm, 1)

            def front(t, i):
                par = t.tt % 2
                if i in CONV_SLOTS:
                    conv_product(t, *divmod(CONV_SLOTS.index(i), TAPS))
                elif i in Z_SLOTS:
                    z_product(t, *divmod(Z_SLOTS.index(i), KM))
                elif i in XD_SLOTS:
                    k = i - XD_SLOTS.start
                    if k == 0:
                        pe.wait_ge(conv_sb, t.count(KI, KI - 1))
                        pe.wait_ge(silu_u, t.count(1, 1))
                    last = pe.matmul(p_mm[0][0:DTR + 2 * NS, :], w_xp[:, k, :], uz[par][:, k, :],
                                     start=k == 0, stop=k == KI - 1)
                    if k == KI - 1:
                        last.then_inc(xd_mm, 1)
                elif i in ROWS_SLOTS:
                    m = ROWS_SLOTS.index(i)
                    if m == 0:
                        pe.wait_ge(conv_sb, t.count(KI, KI))
                        pe.wait_ge(xd_sb, t.count(1, 1))
                    pe.matmul(p_mm[1 - m][:], spread_bc[DTR:DTR + 2 * NS, m, :],
                              xd[DTR:DTR + 2 * NS, :], start=True, stop=True).then_inc(rows_mm, 1)
                elif i in DT_SLOTS:
                    c = DT_SLOTS.index(i)
                    if t is not OPENING or c:
                        pe.wait_ge(dt_sb, t.count(KI, c))
                    pe.matmul(p_dt[:], w_dt[:, c * P:(c + 1) * P], xd[0:DTR, :],
                              start=True, stop=True).then_inc(dt_mm, 1)

            def early(t, i):
                if i in X_SLOTS:
                    x_product(t, *divmod(X_SLOTS.index(i), KM))

            def place(g):
                chunk, quadrant, step = group_place(g)
                return chunk, quadrant // 2, (quadrant % 2) * 4 + step

            def spread_d(t, g):
                chunk, half, which = place(g)
                if g % GC == 0:
                    pe.wait_ge(d_lo, t.count(2 * KI, 2 * chunk + 2))
                if t is not OPENING or g >= 2:
                    pe.wait_ge(decay, t.count(NG, g - 1))
                pe.matmul(p_d[g % 2][:], pick_r[:, which, :], d_parts[:, half, chunk, :],
                          start=True, stop=True).then_inc(d_bc, 1)

            def spread_du(t, g):
                chunk, half, which = place(g)
                if g % GC == 0:
                    pe.wait_ge(du_lo, t.count(2 * KI, 2 * chunk + 2))
                pe.wait_ge(dub, t.count(NG, g + 1))
                pe.matmul(p_du[g % 2][:], pick_r[:, which, :], du_parts[:, half, chunk, :],
                          start=True, stop=True).then_inc(du_bc, 1)

            def fold_quad(t, q):
                chunk, step = divmod(q, 4)
                if step == 0:
                    pe.wait_ge(y_sb, t.count(KI, chunk + 1))
                pe.wait_ge(hc_done, t.count(NG, 4 * q + 4 + HRING))
                for k in range(4):
                    last = pe.matmul(p_y[32 * k:32 * k + 32, :], fold_w[:, step, :],
                                     hc[:, (4 * q + k) % HRING, :], start=step == 0, stop=step == 3,
                                     tile_position=(0, 32 * k))
                last.then_inc(folded, 1)

            def project(t, s, k_first, k_last):
                pe.wait_ge(gated, t.count(KI, k_last + 1))
                if k_first == 0:
                    if s < 2:
                        pe.wait_ge(x_sb, t.following().following().count(KI, 3 + s))
                    else:
                        pe.wait_ge(out_sb, t.count(SUB, s))
                zs = uz[t.tt % 2]
                for k in range(k_first, k_last + 1):
                    last = pe.matmul(p_mm[s % 2][:, 0:DM], zs[:, KI + k, s * P:(s + 1) * P],
                                     w_out[:, k, :], start=k == 0, stop=k == KI - 1)
                if k_last == KI - 1:
                    last.then_inc(out_mm, 1)

            for i in X_SLOTS:
                early(OPENING, i)
            for i in range(FRONT_SLOTS):
                front(OPENING, i)
            for g in range(LEAD):
                spread_d(OPENING, g)
            for g in range(GC):
                spread_du(OPENING, g)
                spread_d(OPENING, g + LEAD)
                early(SECOND, X_SLOTS[0] + g)
                if g % 4 == 1 and g > 5:
                    fold_quad(OPENING, g // 4 - 2)
            with pe.Fori(0, BATCH) as b:
                for tt in range(TILES_B):
                    t = SeqTile(b, tt)
                    nxt = t.following()
                    for i in range(NG):
                        spread_du(*at_group(t, GC + i))
                        for n in decays_of_slot(i):
                            spread_d(*at_group(t, n))
                        front(nxt, i)
                        early(nxt.following(), i)
                        for part in OUT_SLOTS.get(i, ()):
                            project(t, *part)
                        if i % 4 == 1:
                            now, g = at_group(t, GC + i - 8)
                            fold_quad(now, g // 4)
            fold_quad(PAST, 2)
            fold_quad(PAST, 3)

        @block.scalar
        def _(act):
            act.wait_ge(weights_in, 16 * WEIGHTS)
            act.preload_act_table_set(EXP_LN)
            act.activation(a_neg[:], a_neg[:], ACT.Exp).then_inc(a_exp, 1)
            act.wait_ge(consts, 2)
            act.wait_ge(zeroed, 1)
            act.activation(state[:], zeros[:], ACT.Copy).then_inc(saved, 16)

            def front(t, i):
                par = t.tt % 2
                for j in range(KI):
                    if i == Z_SLOTS[KM * j + KM - 1] + 1:
                        act.wait_ge(z_mm, t.count(KI, j + 1))
                        act.activation(uz[par][:, KI + j, :], p_mm[j % 2][:], ACT.Copy).then_inc(z_sb, 1)
                    if i == CONV_SLOTS[TAPS * j + TAPS - 1] + 1:
                        act.wait_ge(conv_mm, t.count(KI, j + 1))
                        act.activation(uz[par][:, j, :], p_mm[j % 2][:], ACT.Identity,
                                       bias=cb[:, j:j + 1]).then_inc(conv_sb, 1)
                if i == SILU_Z_SLOT:
                    act.wait_ge(z_sb, t.count(KI, KI))
                    act.activation(uz[par][:, KI:], uz[par][:, KI:], ACT.Silu).then_inc(silu_z, 1)
                    act.preload_act_table_set(EXP_LN)
                elif i == SILU_U_SLOT:
                    act.wait_ge(conv_sb, t.count(KI, KI))
                    act.activation(uz[par][:, 0:KI], uz[par][:, 0:KI], ACT.Silu).then_inc(silu_u, 1)
                    act.preload_act_table_set(EXP_LN)
                elif i == XD_SLOTS.stop:
                    act.wait_ge(xd_mm, t.count(1, 1))
                    act.activation(xd[:], p_mm[0][0:DTR + 2 * NS, :], ACT.Copy).then_inc(xd_sb, 1)
                elif i - 1 in ROWS_SLOTS:
                    m = ROWS_SLOTS.index(i - 1)
                    act.wait_ge(rows_mm, t.count(2, m + 1))
                    act.activation((b_rows, c_rows)[m][par][:], p_mm[1 - m][:], ACT.Copy).then_inc(rows_sb, 1)
                for c in range(KI):
                    k, step = c % 2, i - DT_SLOTS[c]
                    n = t.count(4 * KI, 4 * c)
                    x_ps = p_dt
                    if step == 1:
                        act.wait_ge(dt_mm, t.count(KI, c + 1))
                        if t is not OPENING or c > 1:
                            act.wait_ge(delta, t.count(KI, c - 1))
                            act.wait_ge(du_lo, t.count(2 * KI, 2 * c - 2))
                        act.activation(sp_e[k][:], x_ps[:], ACT.Abs, bias=dtb[:, c:c + 1]).then_inc(sp_act, 1)
                        act.wait_ge(sp_act, n + 1)
                        act.activation(sp_e[k][:], sp_e[k][:], ACT.Exp, scale=-1.0).then_inc(sp_act, 1)
                    elif step == 2:
                        act.wait_ge(sp_act, n + 2)
                        act.activation(sp_w[k][:], sp_e[k][:], ACT.Identity, bias=1.0).then_inc(sp_act, 1)
                        if t is not OPENING or c:
                            act.wait_ge(sp_dve, t.count(2 * KI, 2 * c))
                        act.activation(sp_l[:], sp_e[k][:], ACT.Ln, bias=1.0).then_inc(sp_act, 1)
                    elif step == 3:
                        act.activation(sp_r[k][:], x_ps[:], ACT.Relu, bias=dtb[:, c:c + 1]).then_inc(dt_sb, 1)
                    elif step == 7:
                        act.wait_ge(delta, t.count(KI, c + 1))
                        if t is not OPENING:
                            act.wait_ge(d_bc, t.count(NG, GC * (c + 1) - NG))
                        split_high(d_parts, sp_r[k], c, d_hi)
                    elif step == 9:
                        act.wait_ge(du, t.count(KI, c + 1))
                        if t is not OPENING:
                            act.wait_ge(du_bc, t.count(NG, GC * (c + 1) - NG))
                        split_high(du_parts, sp_w[k], c, du_hi)

            def early(t, i):
                if i == X_SLOTS[0]:
                    if t.tt == 0:
                        if t is not OPENING:
                            act.wait_ge(conv_mm, SeqTile(t.b, -1).count(KI, KI))
                        act.activation(xb[:, :, 0:TAPS - 1],
                                       zeros[:, 0:KI * (TAPS - 1)].rearrange("p (k w) -> p k w", k=KI),
                                       ACT.Copy).then_inc(halo, 1)
                    else:
                        act.wait_ge(conv_mm, SeqTile(t.b, t.tt - 1).count(KI, KI))
                        act.wait_ge(x_sb, SeqTile(t.b, t.tt - 1).count(KI, KI))
                        act.activation(xb[:, :, 0:TAPS - 1], xb[:, :, NT:NT + TAPS - 1],
                                       ACT.Copy).then_inc(halo, 1)
                for j in range(KI):
                    if i == X_SLOTS[KM * j + KM - 1] + 1:
                        act.wait_ge(halo, t.count(1, 1))
                        act.wait_ge(x_mm, t.count(KI, j + 1))
                        act.activation(xb[:, j, TAPS - 1:], p_mm[j % 2][:], ACT.Copy).then_inc(x_sb, 1)

            def split_high(parts, src, c, done):
                act.activation(parts[0:HALF, 0, c, :], src[0:HALF, :], ACT.Copy).then_inc(done, 1)
                act.activation(parts[HALF:P, 1, c, :], src[HALF:P, :], ACT.Copy).then_inc(done, 1)

            def decay_of(t, g):
                act.wait_ge(d_bc, t.count(NG, g + 1))
                act.wait_ge(scanned, t.count(NG, g + 1))
                act.activation(decays[:, g % DRING, :], p_d[g % 2][:], ACT.Exp,
                               scale=a_neg[:, g:g + 1]).then_inc(decay, 1)

            def save(t, q):
                act.wait_ge(scanned, t.count(NG, 4 * q + 4 + DRING))
                slot = (4 * q) % HRING
                src = (zeros[:, 0:4] if t.tt == TILES_B - 1 else
                       h[:, slot:slot + 4, NT - 1:NT].rearrange("p a b -> p (a b)"))
                act.activation(state[:, 4 * q:4 * q + 4], src, ACT.Copy).then_inc(saved, 1)

            for i in range(X_SLOTS[0], X_SLOTS[-1] + 2):
                early(OPENING, i)
            for i in range(FRONT_SLOTS):
                front(OPENING, i)
            for g in range(LEAD):
                decay_of(OPENING, g)
            for g in range(GC):
                decay_of(OPENING, g + LEAD)
                early(SECOND, X_SLOTS[0] + g)
                if g % 4 == 2 and g > 3:
                    save(OPENING, g // 4 - 1)
            with act.Fori(0, BATCH) as b:
                for tt in range(TILES_B):
                    t = SeqTile(b, tt)
                    nxt = t.following()
                    for i in range(NG):
                        for n in decays_of_slot(i):
                            decay_of(*at_group(t, n))
                        if i % 4 == 2:
                            now, g = at_group(t, GC + i - 4)
                            save(now, g // 4)
                        front(nxt, i)
                        early(nxt.following(), i)

        @block.gpsimd
        def _(pool):
            pool.memset(zeros[:], 0.0).then_inc(zeroed, 1)
            pool.sem_inc(hc_done, HRING)

            def times_c(t, g):
                pool.wait_ge(scanned, t.count(NG, g + 1 + DRING))
                if g == 0:
                    pool.wait_ge(rows_sb, t.count(2, 2))
                if g % 4 == 0:
                    pool.wait_ge(folded, t.count(QUADS, g // 4 + 1))
                s = g % HRING
                pool.tensor_tensor(hc[:, s, :], h[:, s, :], c_rows[t.tt % 2][:], ALU.mult).then_inc(hc_done, 1)

            def front(t, i):
                for c in range(KI):
                    k = c % 2
                    if i == DT_SLOTS[c] + 5:
                        pool.wait_ge(sp_dve, t.count(2 * KI, 2 * c + 2))
                        pool.wait_ge(dt_sb, t.count(KI, c + 1))
                        pool.tensor_tensor(sp_r[k][:], sp_r[k][:], sp_e[k][:], ALU.subtract).then_inc(delta, 1)
                    elif i == DT_SLOTS[c] + 7:
                        pool.wait_ge(delta, t.count(KI, c + 1))
                        pool.wait_ge(silu_u, t.count(1, 1))
                        pool.tensor_tensor(sp_w[k][:], sp_r[k][:], uz[t.tt % 2][:, c, :],
                                           ALU.mult).then_inc(du, 1)

            def gate(t, c):
                pool.wait_ge(y_sb, t.count(KI, c + 1 + 1))
                pool.wait_ge(silu_z, t.count(1, 1))
                zs = uz[t.tt % 2]
                pool.tensor_tensor(zs[:, KI + c, :], zs[:, c, :], zs[:, KI + c, :], ALU.mult).then_inc(gated, 1)

            for i in range(FRONT_SLOTS):
                front(OPENING, i)
            for g in range(1, GC):
                times_c(OPENING, g - 1)
            with pool.Fori(0, BATCH) as b:
                for tt in range(TILES_B):
                    t = SeqTile(b, tt)
                    nxt = t.following()
                    for i in range(NG):
                        times_c(*((t, i + GC - 1) if i <= NG - GC else (nxt, i + GC - 1 - NG)))
                        front(nxt, i)
                        if i % GC == 7:
                            gate(t, i // GC)
            times_c(PAST, GC - 1)

        @block.vector
        def _(dve):
            dve.wait_ge(weights_in, 16 * WEIGHTS)
            ident_sb = uz[1][:, 2, 0:P]
            dve.tensor_copy(pick_r[:], uz[1][:, 0:2, :].rearrange("p a (g m) -> p (a g) m", m=P))
            dve.tensor_copy(spread_bc[:], uz[1][:, 2, P:3 * P].rearrange("p (a m) -> p a m", m=P))
            for j in range(KI):
                for k in range(TAPS):
                    last = dve.tensor_scalar(w_conv[:, j, k, :], ident_sb, taps[:, j, k:k + 1], None, ALU.mult)
            last.then_inc(consts, 1)
            dve.wait_ge(a_exp, 1)
            dve.tensor_scalar(a_neg[:], a_neg[:], -1.0, None, ALU.mult).then_inc(consts, 1)
            dve.memset(res[:], 0.0).then_inc(out_sb, 1)
            dve.sem_inc(scanned, DRING)
            dve.sem_inc(dub, 2)
            dve.sem_inc(y_sb, 1)
            dve.sem_inc(x1_out, 16)

            def times_b(t, g):
                dve.wait_ge(du_bc, t.count(NG, g + 1))
                if g == 0:
                    dve.wait_ge(rows_sb, t.count(2, 2))
                dve.wait_ge(scanned, t.count(NG, g + 1 + DRING - DBRING))
                dve.tensor_tensor(db[:, g % DBRING, :], p_du[g % 2][:], b_rows[t.tt % 2][:],
                                  ALU.mult).then_inc(dub, 1)

            def scan(t, g):
                dve.wait_ge(decay, t.count(NG, g + 1))
                dve.wait_ge(dub, t.count(NG, g + 1 + 2))
                if g % 4 == 0:
                    dve.wait_ge(saved, t.count(QUADS, g // 4 + QUADS - 1))
                dve.wait_ge(hc_done, t.count(NG, g + 1))
                dve.tensor_tensor_scan(h[:, g % HRING, :], decays[:, g % DRING, :], db[:, g % DBRING, :], state[:, g:g + 1],
                                       ALU.mult, ALU.add).then_inc(scanned, 1)

            def front(t, i):
                par = t.tt % 2
                for c in range(KI):
                    k, step = c % 2, i - DT_SLOTS[c]
                    n = t.count(2 * KI, 2 * c)
                    if step == 3:
                        dve.wait_ge(sp_act, t.count(4 * KI, 4 * c + 4))
                        dve.scalar_tensor_tensor(out=sp_w[k][:], in0=sp_w[k][:], scalar=-1.0, in1=sp_l[:],
                                                 op0=ALU.add, op1=ALU.subtract).then_inc(sp_dve, 1)
                    elif step == 4:
                        dve.wait_ge(sp_dve, n + 1)
                        dve.scalar_tensor_tensor(out=sp_e[k][:], in0=sp_w[k][:], scalar=0.0, in1=sp_e[k][:],
                                                 op0=ALU.max, op1=ALU.subtract).then_inc(sp_dve, 1)
                    elif step == 8:
                        dve.wait_ge(d_hi, t.count(2 * KI, 2 * c + 2))
                        split_low(d_parts, sp_r[k], c, d_lo)
                    elif step == 10:
                        dve.wait_ge(du_hi, t.count(2 * KI, 2 * c + 2))
                        split_low(du_parts, sp_w[k], c, du_lo)

            def split_low(parts, src, c, done):
                dve.tensor_tensor(parts[HALF:P, 0, c, :], src[0:HALF, :],
                                  parts[0:HALF, 0, c, :].bitcast(F32), ALU.subtract).then_inc(done, 1)
                dve.tensor_tensor(parts[0:HALF, 1, c, :], src[HALF:P, :],
                                  parts[HALF:P, 1, c, :].bitcast(F32), ALU.subtract).then_inc(done, 1)

            def skip(t, c):
                u = uz[t.tt % 2][:, c, :]
                dve.wait_ge(folded, t.count(QUADS, 4 * c + 4 + 2))
                dve.scalar_tensor_tensor(out=u, in0=u, scalar=dpar[:, c:c + 1], in1=p_y[:],
                                         op0=ALU.mult, op1=ALU.add).then_inc(y_sb, 1)

            def residual(t, s):
                dve.wait_ge(out_mm, t.count(SUB, s + 1))
                if s == 0:
                    dve.wait_ge(x_in, t.count(16, 16))
                dve.tensor_tensor(res[:, s, :], p_mm[s % 2][:, 0:DM], x_nat[:, s, :], ALU.add).then_inc(out_sb, 1)

            N_LN = 2 * SUB + 1 + N_RSTD
            STATS_SLOT, AGGR_SLOT, RSTD_SLOT = 1, 5, 6
            SCALE_SLOT = 29

            def norm(t, i):
                def done(n):
                    dve.wait_ge(ln_dve, t.count(N_LN, n))

                if STATS_SLOT <= i < STATS_SLOT + SUB:
                    s = i - STATS_SLOT
                    if s == 0:
                        dve.wait_ge(out_sb, t.count(SUB, 1))
                    dve.bn_stats(stats[:, s, :], res[:, s, :]).then_inc(ln_dve, 1)
                elif i == AGGR_SLOT:
                    done(SUB)
                    dve.sem_inc(waited, 1)
                    for s in range(SUB):
                        dve.bn_aggr(mv[:, s, :], stats[:, s, :]).then_inc(ln_dve, 1)
                elif i == RSTD_SLOT:
                    done(2 * SUB)
                    dve.tensor_copy(var4[:], mv[:, :, 1:2].rearrange("p a b -> p (a b)")).then_inc(ln_dve, 1)
                elif RSTD_SLOT < i <= RSTD_SLOT + N_RSTD:
                    n = i - RSTD_SLOT - 1
                    done(2 * SUB + 1 + n)
                    rstd_step(dve, n, var4, y4, a4).then_inc(ln_dve, 1)
                elif SCALE_SLOT <= i < SCALE_SLOT + SUB:
                    s = i - SCALE_SLOT
                    done(N_LN)
                    dve.tensor_scalar(res[:, s, :], res[:, s, :], mv[:, s, 0:1], y4[:, s:s + 1],
                                      ALU.subtract, ALU.mult).then_inc(ln_out, 1)

            for i in range(FRONT_SLOTS):
                front(OPENING, i)
            for g in range(GC):
                times_b(OPENING, g)
                if g:
                    scan(OPENING, g - 1)
            with dve.Fori(0, BATCH) as b:
                for tt in range(TILES_B):
                    t = SeqTile(b, tt)
                    nxt = t.following()
                    for i in range(NG):
                        times_b(*at_group(t, GC + i))
                        norm(t, i)
                        scan(*at_group(t, GC + i - 1))
                        front(nxt, i)
                        if i % GC == 6:
                            skip(t, i // GC)
                        if i in SUM_SLOTS:
                            if i == SUM_SLOTS[0]:
                                dve.wait_ge(ln_out, t.count(SUB, SUB))
                                dve.wait_ge(x1_out, t.count(16, 16))
                            residual(t, SUM_SLOTS.index(i))
            for i in range(SCALE_SLOT + SUB):
                norm(PAST, i)
            scan(PAST, GC - 1)


W_COLS = (2 * KM + 2 * KH) * DH + KH * DM
W1_AT, W2_AT, H1_AT, H2_AT, W3_AT = 0, KM * DH, 2 * KM * DH, (2 * KM + KH) * DH, (2 * KM + 2 * KH) * DH


def ffn_stage(nc, sems, ctx, split, branch, weights, x1, scales, s3, ident, out):
    tag = "s_" if split else "g_"
    WT = F32R if split else F32
    parts = 2 if split else 1

    def sb(name, shape, dt=F32):
        return ctx.enter_context(nc.sbuf_tensor(tag + name, shape, dt))

    def sem(name):
        return sems.enter_context(nc.semaphore(tag + name))

    x_nat = [sb(f"x_nat{i}", [P, SUB, DM]) for i in range(2)]
    x_t = [[sb(f"x_t{i}{j}", [P, KM, NT], WT) for j in range(parts)] for i in range(2)]
    acts = [[sb(f"act{i}{j}", [P, KH, NT], WT) for j in range(parts)] for i in range(2)]
    hring = [sb(f"h{i}", [P, NT]) for i in range(3)] if split else None
    silu_t = [sb(f"silu{i}", [P, NT]) for i in range(2)]
    res = sb("res", [P, SUB, DM])
    sc = sb("sc", [P, 4, KH])
    s3b = sb("s3b", [P, DM])
    idn = sb("idn", [P, P])
    stats = sb("stats", [P, SUB, 6])
    mv = sb("mv", [P, SUB, 2])
    var4, y4, a4 = sb("var4", [P, SUB]), sb("y4", [P, SUB]), sb("a4", [P, SUB])
    bank = [ctx.enter_context(nc.psum_tensor(f"{tag}bank{i}", [P, NT], F32)) for i in range(8)]
    p_w1, p_w2, p_h, p_o = bank[0:2], bank[2:4], bank[4:6], bank[6:8]

    consts_in, stored = sem("consts_in"), sem("stored")
    x_in = [sem("x_in0"), sem("x_in1")]
    tr_mm, w1_mm, w2_mm, h_mm, o_mm = (sem(s) for s in ("tr_mm", "w1_mm", "w2_mm", "h_mm", "o_mm"))
    xt_hi, xt_lo = sem("xt_hi"), sem("xt_lo")
    silu, gate, gelu = sem("silu"), sem("gate"), sem("gelu")
    hi, lo = sem("hi"), sem("lo")
    scaled, summed = sem("scaled"), sem("summed")
    ln_dve, ln_out = sem("ln_dve"), sem("ln_out")
    waited = sem("waited")
    STEPS = TILES // PairTile.OF_STEP
    first = PairTile(0, 0)
    L3 = 3 * KH

    block = ctx.enter_context(nc.Block())

    @block.sync
    def _(sp):
        def body():
            for k in range(4):
                sp.dma_start(sc[:, k, :], scales[k]).then_inc(consts_in, 16)
            sp.dma_start(s3b[:], s3).then_inc(consts_in, 16)
            sp.dma_start(idn[:], ident).then_inc(consts_in, 16)

            def load(t):
                row = t.b * (2 * NT) + t.tt * NT
                if t is not first:
                    row = row % (BATCH * SEQ)
                sp.dma_start(x_nat[t.tt][:], x1[bass.ds(row, NT), :].rearrange("(s p) c -> p s c", p=P))\
                  .then_inc(x_in[t.tt], 16)

            load(first)
            with sp.Fori(0, STEPS) as b:
                for tt in range(2):
                    t = PairTile(b, tt)
                    sp.wait_ge(summed, t.count(SUB, SUB))
                    sp.sem_inc(waited, 1)
                    load(t.following())
                    sp.wait_ge(ln_out, t.count(SUB, SUB))
                    sp.sem_inc(waited, 1)
                    sp.dma_start(out[bass.ds(b * (2 * NT) + tt * NT, NT), :]
                                 .rearrange("(s p) c -> p s c", p=P), res[:]).then_inc(stored, 16)
            sp.wait_ge(stored, 16 * TILES + 16)
        branch(sp, body)

    @block.tensor
    def _(pe):
        def body():
            pe.wait_ge(consts_in, 16 * 6)

            def product(dst, n_k, w_at, ins, rows_w, cols, wait=None):
                for k in range(n_k):
                    if wait:
                        wait(k)
                    for j in range(parts):
                        last = pe.matmul(dst, weights[:, w_at + k * rows_w + cols:w_at + k * rows_w + cols + P],
                                         ins[j][:, k, :], start=k == 0 and j == 0,
                                         stop=k == n_k - 1 and j == parts - 1)
                return last

            def transposes(t):
                pe.wait_ge(x_in[t.tt], t.b * 16 + 16)
                for k in range(KM):
                    if t is not first:
                        pe.wait_ge(scaled, PairTile(t.b, t.tt - 1).count(SUB, SUB))
                    for s in range(SUB):
                        last = pe.transpose(p_o[k][:, s * P:(s + 1) * P], x_nat[t.tt][:, s, k * P:(k + 1) * P],
                                            idn[:])
                    last.then_inc(tr_mm, 1)

            def gated(t):
                pe.wait_ge(xt_lo if split else xt_hi, t.count(KM, KM))
                for m in range(KH):
                    pe.wait_ge(silu, t.count(KH, m + 1))
                    product(p_w1[m % 2][:], KM, W1_AT, x_t[t.tt], DH, m * P).then_inc(w1_mm, 1)
                    pe.wait_ge(gate, t.count(KH, m + 1))
                    product(p_w2[m % 2][:], KM, W2_AT, x_t[t.tt], DH, m * P).then_inc(w2_mm, 1)

            def hidden(t, layer):
                w_at = (H1_AT, H2_AT)[layer]
                done = lo if split else (gate, gelu)[layer]

                def arrived(k):
                    if split:
                        pe.wait_ge(lo, t.count(L3, layer * KH + k + 1))
                    elif layer == 0:
                        pe.wait_ge(gate, t.count(KH, k + 1 + 2))
                    else:
                        pe.wait_ge(gelu, t.count(2 * KH, k + 1 + 2))
                for m in range(KH):
                    pe.wait_ge(gelu, t.count(2 * KH, layer * KH + m + 1))
                    product(p_h[m % 2][:], KH, w_at, acts[layer], DH, m * P,
                            arrived if m == 0 else None).then_inc(h_mm, 1)
                    if layer == 1 and m == 3:
                        transposes(t.following())

            def output(t):
                for s in range(SUB):
                    if s < 2:
                        nxt = t.following()
                        pe.wait_ge(xt_lo if split else xt_hi, nxt.count(KM, s + 1))
                    else:
                        pe.wait_ge(scaled, t.count(SUB, s - 1 + 4))
                    for k in range(KH):
                        if s == 0:
                            if split:
                                pe.wait_ge(lo, t.count(L3, 2 * KH + k + 1))
                            else:
                                pe.wait_ge(gelu, t.count(2 * KH, KH + k + 1 + 2))
                        for j in range(parts):
                            last = pe.matmul(p_o[s % 2][:, 0:DM], acts[0][j][:, k, s * P:(s + 1) * P],
                                             weights[:, W3_AT + k * DM:W3_AT + (k + 1) * DM],
                                             start=k == 0 and j == 0, stop=k == KH - 1 and j == parts - 1)
                    last.then_inc(o_mm, 1)

            transposes(first)
            gated(first)
            with pe.Fori(0, STEPS) as b:
                for tt in range(2):
                    t = PairTile(b, tt)
                    hidden(t, 0)
                    hidden(t, 1)
                    output(t)
                    gated(t.following())
        branch(pe, body)

    @block.scalar
    def _(act):
        def body():
            act.wait_ge(consts_in, 16 * 6)
            act.sem_inc(silu, 2)
            act.sem_inc(gelu, 2)

            def transposed(t):
                for k in range(KM):
                    act.wait_ge(tr_mm, t.count(KM, k + 1))
                    act.activation(x_t[t.tt][0][:, k, :], p_o[k][:], ACT.Copy).then_inc(xt_hi, 1)

            def high(t, c):
                if c < KH:
                    act.wait_ge(gate, t.count(KH, c + 1 + 2))
                else:
                    act.wait_ge(gelu, t.count(2 * KH, c - KH + 1 + 2))
                act.activation(acts[(c // KH) % 2][0][:, c % KH, :], hring[c % 3][:], ACT.Copy).then_inc(hi, 1)

            def gated(t):
                for m in range(KH):
                    act.wait_ge(w1_mm, t.count(KH, m + 1))
                    if m > 1 or t is not first:
                        act.wait_ge(gate, t.count(KH, m - 2 + 1 + 2))
                    act.activation(silu_t[m % 2][:], p_w1[m % 2][:], ACT.Silu,
                                   scale=sc[:, 0, m:m + 1]).then_inc(silu, 1)
                    if split and m:
                        high(t, m - 1)
                if split:
                    high(t, KH - 1)

            def hidden(t, layer):
                for m in range(KH):
                    c = (layer + 1) * KH + m
                    act.wait_ge(h_mm, t.count(2 * KH, layer * KH + m + 1))
                    if split:
                        act.wait_ge(lo, t.count(L3, c - 2))
                        dst = hring[c % 3][:]
                    else:
                        dst = acts[1 - layer][0][:, m, :]
                    act.activation(dst, p_h[m % 2][:], ACT.Gelu,
                                   scale=sc[:, 2 + layer, m:m + 1]).then_inc(gelu, 1)
                    if split:
                        high(t, c)
                    if layer == 1 and m == 4:
                        transposed(t.following())

            transposed(first)
            gated(first)
            with act.Fori(0, STEPS) as b:
                for tt in range(2):
                    t = PairTile(b, tt)
                    hidden(t, 0)
                    hidden(t, 1)
                    gated(t.following())
        branch(act, body)

    @block.vector
    def _(dve):
        def body():
            dve.wait_ge(consts_in, 16 * 6)
            dve.sem_inc(gate, 2)
            dve.sem_inc(scaled, 4)
            dve.sem_inc(summed, 4)
            dve.sem_inc(stored, 16)

            def transposed(t):
                if split:
                    for k in range(KM):
                        dve.wait_ge(xt_hi, t.count(KM, k + 1))
                        dve.tensor_tensor(x_t[t.tt][1][:, k, :], p_o[k][:], x_t[t.tt][0][:, k, :].bitcast(F32),
                                          ALU.subtract).then_inc(xt_lo, 1)

            def low(t, c):
                a = acts[(c // KH) % 2]
                dve.wait_ge(hi, t.count(L3, c + 1))
                dve.tensor_tensor(a[1][:, c % KH, :], hring[c % 3][:], a[0][:, c % KH, :].bitcast(F32),
                                  ALU.subtract).then_inc(lo, 1)

            def gated(t):
                for m in range(KH):
                    dve.wait_ge(w2_mm, t.count(KH, m + 1))
                    dve.wait_ge(silu, t.count(KH, m + 1 + 2))
                    if split and (m > 2 or t is not first):
                        dve.wait_ge(lo, t.count(L3, m - 2))
                    dst = hring[m % 3][:] if split else acts[0][0][:, m, :]
                    dve.scalar_tensor_tensor(out=dst, in0=p_w2[m % 2][:], scalar=sc[:, 1, m:m + 1],
                                             in1=silu_t[m % 2][:], op0=ALU.mult, op1=ALU.mult).then_inc(gate, 1)
                    if split and m:
                        low(t, m - 1)
                if split:
                    low(t, KH - 1)

            def hidden(t, layer):
                for m in range(KH):
                    if split:
                        low(t, (layer + 1) * KH + m)
                    if layer == 1 and m == 4:
                        transposed(t.following())

            def residual(t):
                for s in range(SUB):
                    dve.wait_ge(o_mm, t.count(SUB, s + 1))
                    if s == 0:
                        dve.wait_ge(stored, t.count(16, 16))
                    dve.tensor_tensor(res[:, s, :], p_o[s % 2][:, 0:DM], s3b[:], ALU.mult).then_inc(scaled, 1)
                    dve.wait_ge(scaled, t.count(SUB, s + 1 + 4))
                    dve.tensor_tensor(res[:, s, :], res[:, s, :], x_nat[t.tt][:, s, :], ALU.add).then_inc(summed, 1)

            N_LN = 2 * SUB + 1 + 3 + 16

            def norm(t):
                count = [2 * SUB]

                def link(ins):
                    count[0] += 1
                    ins.then_inc(ln_dve, 1)
                    dve.wait_ge(ln_dve, t.count(N_LN, count[0]))

                dve.wait_ge(summed, t.count(SUB, SUB + 4))
                for s in range(SUB):
                    dve.bn_stats(stats[:, s, :], res[:, s, :]).then_inc(ln_dve, 1)
                dve.wait_ge(ln_dve, t.count(N_LN, SUB))
                dve.sem_inc(waited, 1)
                for s in range(SUB):
                    dve.bn_aggr(mv[:, s, :], stats[:, s, :]).then_inc(ln_dve, 1)
                dve.wait_ge(ln_dve, t.count(N_LN, 2 * SUB))
                link(dve.tensor_copy(var4[:], mv[:, :, 1:2].rearrange("p a b -> p (a b)")))
                for n in range(N_RSTD):
                    link(rstd_step(dve, n, var4, y4, a4))
                for s in range(SUB):
                    dve.tensor_scalar(res[:, s, :], res[:, s, :], mv[:, s, 0:1], y4[:, s:s + 1],
                                      ALU.subtract, ALU.mult).then_inc(ln_out, 1)

            transposed(first)
            gated(first)
            with dve.Fori(0, STEPS) as b:
                for tt in range(2):
                    t = PairTile(b, tt)
                    hidden(t, 0)
                    hidden(t, 1)
                    residual(t)
                    gated(t.following())
                    norm(t)
        branch(dve, body)


def weight_pieces(a):
    for name in ("w1T", "w2T", "h1T", "h2T", "w3T"):
        w = a[name]
        for k in range(w.shape[0] // P):
            yield w[k * P:(k + 1) * P, :]


def round_weights(nc, sems, ctx, a, flag):
    pieces = list(weight_pieces(a))
    n, ring = len(pieces), 4
    cols = [piece.shape[1] for piece in pieces]
    at = [sum(cols[:i]) for i in range(n)]
    weights = ctx.enter_context(nc.sbuf_tensor("weights_r", [P, W_COLS], F32R))
    with ExitStack() as own:
        stage = [own.enter_context(nc.sbuf_tensor(f"stage{i}", [P, DH], F32)) for i in range(ring)]
        lost = [own.enter_context(nc.sbuf_tensor(f"lost{i}", [P, DH], F32)) for i in range(2)]
        worst = own.enter_context(nc.sbuf_tensor("worst", [P, n], F32))
        top = own.enter_context(nc.sbuf_tensor("top", [P, 1], F32))
        exact = own.enter_context(nc.sbuf_tensor("exact", [P, 1], F32))
        ones = own.enter_context(nc.sbuf_tensor("ones", [P, 1], F32))
        total = own.enter_context(nc.psum_tensor("total", [P, 1], F32))
        loaded = [sems.enter_context(nc.semaphore(f"w_loaded{i}")) for i in range(ring)]
        rounded, measured, took, counted, checked, flag_out = (
            sems.enter_context(nc.semaphore(s)) for s in
            ("w_rounded", "w_measured", "w_took", "w_counted", "w_checked", "flag_out"))
        with nc.Block() as block:
            @block.sync
            def _(sp):
                for i, piece in enumerate(pieces):
                    if i >= ring:
                        sp.wait_ge(took, i - ring + 1)
                    sp.dma_start(stage[i % ring][:, 0:cols[i]], piece).then_inc(loaded[i % ring], 16)

            @block.scalar
            def _(act):
                for i in range(n):
                    act.wait_ge(loaded[i % ring], 16 * (i // ring + 1))
                    act.activation(weights[:, at[i]:at[i] + cols[i]], stage[i % ring][:, 0:cols[i]],
                                   ACT.Copy).then_inc(rounded, 1)

            @block.vector
            def _(dve):
                dve.memset(ones[:], 1.0)
                for i in range(n + 1):
                    if i < n:
                        dve.wait_ge(rounded, i + 1)
                        if i >= 2:
                            dve.wait_ge(measured, i - 1)
                        dve.tensor_tensor(lost[i % 2][:, 0:cols[i]], stage[i % ring][:, 0:cols[i]],
                                          weights[:, at[i]:at[i] + cols[i]].bitcast(F32),
                                          ALU.not_equal).then_inc(took, 1)
                    if i:
                        dve.wait_ge(took, i)
                        dve.tensor_reduce(worst[:, i - 1:i], lost[(i - 1) % 2][:, 0:cols[i - 1]],
                                          mybir.AxisListType.X, ALU.max).then_inc(measured, 1)
                dve.wait_ge(measured, n)
                dve.tensor_reduce(top[:], worst[:], mybir.AxisListType.X, ALU.max).then_inc(measured, 1)
                dve.wait_ge(measured, n + 1)
                dve.tensor_scalar(exact[:], top[:], 0.0, None, ALU.is_equal).then_inc(measured, 1)
                dve.wait_ge(counted, 1)
                dve.tensor_scalar(flag[0:1, 0:1], total[0:1, :], float(P), None,
                                  ALU.is_equal).then_inc(checked, 1)

            @block.tensor
            def _(pe):
                pe.wait_ge(measured, n + 2)
                pe.matmul(total[0:1, :], ones[:], exact[:], start=True, stop=True).then_inc(counted, 1)
    return weights


def load_float32_weights(nc, sems, ctx, a, branch):
    weights = ctx.enter_context(nc.sbuf_tensor("weights_f32", [P, W_COLS], F32))
    loaded = sems.enter_context(nc.semaphore("weights_f32_in"))
    with nc.Block() as block:
        @block.sync
        def _(sp):
            def body():
                at = n = 0
                for piece in weight_pieces(a):
                    sp.dma_start(weights[:, at:at + piece.shape[1]], piece).then_inc(loaded, 16)
                    at += piece.shape[1]
                    n += 1
                sp.wait_ge(loaded, 16 * n)
            branch(sp, body)
    return weights


def program(nc, a, x1, out):
    with ExitStack() as sems:
        mamba_stage(nc, sems, a["xT"], a["x"], a["in_wT"], a["conv_w"], a["conv_b"], a["xp_wT"], a["dt_wT"],
                    a["dt_b"], a["A_log"], a["D_param"], a["out_wT"], a["pick"], a["fold"], a["ident"], x1)
        x1_rows, out_rows = (v.rearrange("b l c -> (b l) c") for v in (x1, out))
        scales = [a["s1"], a["s2"], a["sh1"], a["sh2"]]
        ident = a["ident"][:, 0:1, :].rearrange("p a m -> p (a m)")
        flag = sems.enter_context(nc.sbuf_tensor("flag", [P, 1], I32))

        def when(value):
            def branch(eng, body):
                exact = eng.value_load(flag[0:1, 0:1], min_val=0, max_val=1)
                with eng.If(exact == value):
                    body()
            return branch

        with ExitStack() as ctx:
            weights = round_weights(nc, sems, ctx, a, flag)
            ffn_stage(nc, sems, ctx, True, when(1), weights, x1_rows, scales, a["s3"], ident, out_rows)
        with ExitStack() as ctx:
            weights = load_float32_weights(nc, sems, ctx, a, when(0))
            ffn_stage(nc, sems, ctx, False, when(0), weights, x1_rows, scales, a["s3"], ident, out_rows)


def shape_constants():
    pick = np.zeros((P, HALF // GD, P), np.float32)
    fold = np.zeros((P, 4, 32), np.float32)
    ident = np.zeros((P, 3, P), np.float32)
    ident[:, 0] = np.eye(P)
    for d in range(GD):
        for n in range(NS):
            row = d * NS + n
            for which in range(HALF // GD):
                pick[which * GD + d, which, row] = 1
                pick[HALF + which * GD + d, which, row] = 1
            for step in range(4):
                fold[row, step, step * GD + d] = 1
            ident[DTR + n, 1, row] = 1
            ident[DTR + NS + n, 2, row] = 1
    return pick, fold, ident


def kernel(**inputs):
    import concourse.bacc as bacc
    from concourse.bass_utils import run_bass_kernel_spmd

    v = {k.removeprefix("L0_"): np.asarray(x) for k, x in inputs.items()}
    pick, fold, ident = shape_constants()

    def column(x):
        return np.ascontiguousarray(x.reshape(-1, P).T)

    a_log = v["attn_A_log"].reshape(KI, 4, 4, GD, NS).transpose(3, 4, 0, 2, 1).reshape(P, NG)
    arrays = {
        "x": v["attn_hidden_states"],
        "xT": v["attn_hidden_states"].transpose(0, 2, 1),
        "in_wT": v["attn_in_proj_w"].T, "conv_w": v["attn_conv_w"], "conv_b": column(v["attn_conv_b"]),
        "xp_wT": v["attn_x_proj_w"].T, "dt_wT": v["attn_dt_proj_w"].T, "dt_b": column(v["attn_dt_proj_b"]),
        "A_log": a_log, "D_param": column(v["attn_D_param"]), "out_wT": v["attn_out_proj_w"].T,
        "pick": pick, "fold": fold, "ident": ident,
        "w1T": v["ffn_w1_w"].T, "w2T": v["ffn_w2_w"].T, "h1T": v["ffn_h1_w"].T, "h2T": v["ffn_h2_w"].T,
        "w3T": v["ffn_w3_w"].T,
        "s1": column(v["ffn_w1_s"]), "s2": column(v["ffn_w2_s"]), "sh1": column(v["ffn_h1_s"]),
        "sh2": column(v["ffn_h2_s"]), "s3": np.broadcast_to(v["ffn_w3_s"], (P, DM)),
    }
    arrays = {k: np.ascontiguousarray(x) for k, x in arrays.items()}
    nc = bacc.Bacc("TRN2", target_bir_lowering=False, num_devices=1)
    aps = {k: nc.dram_tensor(f"in_{k}", x.shape, mybir.dt.from_np(x.dtype), kind="ExternalInput").ap()
           for k, x in arrays.items()}
    x1 = nc.dram_tensor("x1", (BATCH, SEQ, DM), F32, kind="Internal").ap()
    out = nc.dram_tensor("out", (BATCH, SEQ, DM), F32, kind="ExternalOutput").ap()
    program(nc, aps, x1, out)
    r = run_bass_kernel_spmd(nc, [{f"in_{k}": x for k, x in arrays.items()}], core_ids=[0])
    return r.results[0]["out"]
```

```python
import concourse.bass as bass
from concourse import mybir
from contextlib import ExitStack
import numpy as np

F32 = mybir.dt.float32
F32R = mybir.dt.float32r
BF16 = mybir.dt.bfloat16
I32 = mybir.dt.int32
ALU = mybir.AluOpType
ACT = mybir.ActivationFunctionType

P = 128
BATCH, SEQ, DM = 4, 2048, 256
DI, NS, DTR, TAPS = 512, 16, 64, 4
DH = 1024
NT = 512
TILES_B = SEQ // NT
TILES = BATCH * TILES_B
KM, KI, KH = DM // P, DI // P, DH // P
SUB = NT // P
GD = P // NS
NG = DI // GD
GC = P // GD
QUADS = NG // 4
HALF = P // 2
HRING = 8
EPS = 1e-5
EXP_LN = "natural_log_exp_and_others"
RSQRT_SEED = float(0x5F3759DF)


def group_place(g):
    chunk, k = divmod(g, GC)
    quadrant, step = k % 4, k // 4
    return chunk, quadrant, step


class Tile:

    def __init__(self, b, tt):
        self.b, self.tt = b, tt

    def count(self, per_tile, n):
        return self.b * (self.OF_STEP * per_tile) + (self.tt * per_tile + n)

    def following(self):
        if self.tt + 1 < self.OF_STEP:
            return type(self)(self.b, self.tt + 1)
        return type(self)(self.b + 1, 0)


class SeqTile(Tile):
    OF_STEP = TILES_B


class PairTile(Tile):
    OF_STEP = 2


CONV_SLOTS = [i for i in range(KI * (TAPS + 1)) if i % (TAPS + 1) > 0]
SILU_U_SLOT = CONV_SLOTS[-1] + 1
XD_SLOTS = range(27, 27 + KI)
ROWS_SLOTS, DT_SLOTS = (XD_SLOTS.stop + 1, XD_SLOTS.stop + 3), (33, 38, 43, 48)
BETWEEN = [i for i in range(DT_SLOTS[0] + 4, NG) if i not in DT_SLOTS]
Z_SLOTS, X_SLOTS = BETWEEN[:KI * KM], BETWEEN[KI * KM:2 * KI * KM]
SILU_Z_SLOT = 58
FRONT_SLOTS = DT_SLOTS[-1] + 11
OUT_SLOTS = {57: ((0, 0, 2),), 58: ((1, 0, 2),), 59: ((0, 3, 3), (1, 3, 3)), 61: ((2, 0, 3),), 62: ((3, 0, 3),)}
SUM_SLOTS = (59, 60, 62, 63)
LEAD = 4
HOLD = {SILU_U_SLOT: 3, SILU_Z_SLOT: 2}
DRING, DBRING = 8, 4


def at_group(t, n):
    return (t, n) if n < NG else (t.following(), n - NG)


def decays_of_slot(i):
    for silu, hold in HOLD.items():
        if silu < i <= silu + hold:
            return ()
        if silu + hold < i <= silu + 2 * hold:
            n = GC + LEAD + silu + 1 + 2 * (i - silu - hold - 1)
            return n, n + 1
    return (GC + LEAD + i,)


OPENING = SeqTile(0, 0)
SECOND = SeqTile(0, 1)
LAST_ROW = [SeqTile(BATCH - 1, tt) for tt in range(TILES_B)]


def exists(t):
    return not isinstance(t.b, int) or t.b < BATCH
PAST = SeqTile(BATCH, 0)


N_RSTD = 3 + 4 * 4


def rstd_step(dve, n, var4, y4, a4):
    if n == 0:
        return dve.tensor_scalar(var4[:], var4[:], EPS, None, ALU.add)
    if n == 1:
        return dve.tensor_scalar(a4[:].bitcast(I32), var4[:].bitcast(I32), 1, None, ALU.logical_shift_right)
    if n == 2:
        return dve.tensor_scalar(y4[:].bitcast(I32), a4[:].bitcast(I32), -1.0, RSQRT_SEED, ALU.mult, ALU.add)
    if n % 4 == 3:
        return dve.tensor_tensor(a4[:], y4[:], y4[:], ALU.mult)
    if n % 4 == 0:
        return dve.tensor_tensor(a4[:], a4[:], var4[:], ALU.mult)
    if n % 4 == 1:
        return dve.tensor_scalar(a4[:], a4[:], -0.5, 1.5, ALU.mult, ALU.add)
    return dve.tensor_tensor(y4[:], y4[:], a4[:], ALU.mult)


def mamba_stage(nc, sems, xT, x, in_wT, conv_w, conv_b, xp_wT, dt_wT, dt_b, A_log, D_param, out_wT,
                pick, fold, ident, x1):
    ctx = ExitStack()
    with ctx:
        def sb(name, shape, dt=F32):
            return ctx.enter_context(nc.sbuf_tensor(name, shape, dt))

        def sem(name):
            return sems.enter_context(nc.semaphore(name))

        w_in = sb("w_in", [P, KM, 2 * DI])
        w_xp = sb("w_xp", [P, KI, DTR + 2 * NS])
        w_dt = sb("w_dt", [DTR, DI])
        w_out = sb("w_out", [P, KI, DM])
        w_conv = sb("w_conv", [P, KI, TAPS, P])
        pick_r = sb("pick_r", [P, HALF // GD, P], F32R)
        fold_w = sb("fold_w", [P, 4, 32])
        spread_bc = sb("spread_bc", [P, 2, P])
        taps = sb("taps", [P, KI, TAPS])
        cb = sb("cb", [P, KI])
        dtb = sb("dtb", [P, KI])
        dpar = sb("dpar", [P, KI])
        a_neg = sb("a_neg", [P, NG])
        zeros = sb("zeros", [P, NG])
        xT_sb = [sb(f"xT_sb{i}", [P, KM, NT]) for i in range(2)]
        x_nat = sb("x_nat", [P, SUB, DM])
        res = sb("res", [P, SUB, DM])
        xb = sb("xb", [P, KI, TAPS - 1 + NT])
        uz = [sb(f"uz{i}", [P, 2 * KI, NT]) for i in range(2)]
        d_parts = sb("d_parts", [P, 2, KI, NT], F32R)
        du_parts = sb("du_parts", [P, 2, KI, NT], F32R)
        b_rows = [sb(f"b_rows{i}", [P, NT]) for i in range(2)]
        c_rows = [sb(f"c_rows{i}", [P, NT]) for i in range(2)]
        sp_e = [sb(f"sp_e{i}", [P, NT]) for i in range(2)]
        sp_w = [sb(f"sp_w{i}", [P, NT]) for i in range(2)]
        sp_l = sb("sp_l", [P, NT])
        sp_r = [sb(f"sp_r{i}", [P, NT]) for i in range(2)]
        decays = sb("decays", [P, DRING, NT])
        db = sb("db", [P, DBRING, NT])
        h = sb("h", [P, HRING, NT])
        hc = sb("hc", [P, HRING, NT])
        state = sb("state", [P, NG])
        stats = sb("stats", [P, SUB, 6])
        mv = sb("mv", [P, SUB, 2])
        var4 = sb("var4", [P, SUB])
        y4 = sb("y4", [P, SUB])
        a4 = sb("a4", [P, SUB])
        xd = sb("xd", [DTR + 2 * NS, NT])

        bank = [ctx.enter_context(nc.psum_tensor(f"bank{i}", [P, NT], F32)) for i in range(8)]
        p_mm, p_dt, p_d, p_du, p_y = bank[0:2], bank[2], bank[3:5], bank[5:7], bank[7]

        weights_in = sem("weights_in")
        zeroed = sem("zeroed")
        a_exp = sem("a_exp")
        consts = sem("consts")
        xT_in, x_in, x1_out = sem("xT_in"), sem("x_in"), sem("x1_out")
        x_mm, z_mm, conv_mm, xd_mm, rows_mm, dt_mm, out_mm = (
            sem(s) for s in ("x_mm", "z_mm", "conv_mm", "xd_mm", "rows_mm", "dt_mm", "out_mm"))
        x_sb, z_sb, conv_sb, xd_sb, rows_sb, dt_sb, out_sb = (
            sem(s) for s in ("x_sb", "z_sb", "conv_sb", "xd_sb", "rows_sb", "dt_sb", "out_sb"))
        halo, silu_u, silu_z = sem("halo"), sem("silu_u"), sem("silu_z")
        sp_act = sem("sp_act")
        sp_dve = sem("sp_dve")
        delta = sem("delta")
        d_hi, d_lo, du, du_hi, du_lo = (sem(s) for s in ("d_hi", "d_lo", "du", "du_hi", "du_lo"))
        d_bc, du_bc = sem("d_bc"), sem("du_bc")
        decay = sem("decay")
        dub = sem("dub")
        scanned = sem("scanned")
        saved = sem("saved")
        hc_done = sem("hc_done")
        folded = sem("folded")
        y_sb, gated = sem("y_sb"), sem("gated")
        ln_dve, ln_out = sem("ln_dve"), sem("ln_out")
        waited = sem("waited")

        block = ctx.enter_context(nc.Block())

        WEIGHTS = 12

        @block.sync
        def _(sp):
            for dst, src in (
                (w_in[:], in_wT.rearrange("(k p) e -> p k e", p=P)),
                (w_xp[:], xp_wT.rearrange("(k p) e -> p k e", p=P)),
                (w_dt[:], dt_wT),
                (w_out[:], out_wT.rearrange("(k p) e -> p k e", p=P)),
                (taps[:], conv_w.rearrange("(k p) w -> p k w", p=P)),
                (cb[:], conv_b),
                (dtb[:], dt_b),
                (dpar[:], D_param),
                (a_neg[:], A_log),
                (fold_w[:], fold),
                (uz[1][:, 0:2, :].rearrange("p a (g m) -> p (a g) m", m=P), pick),
                (uz[1][:, 2, 0:3 * P].rearrange("p (a m) -> p a m", m=P), ident),
            ):
                sp.dma_start(dst, src).then_inc(weights_in, 16)

            def load_xT(t):
                sp.dma_start(xT_sb[t.tt % 2][:], xT[t.b, :, t.tt * NT:(t.tt + 1) * NT]
                             .rearrange("(k p) t -> p k t", p=P)).then_inc(xT_in, 16)

            load_xT(OPENING)
            sp.wait_ge(x_mm, KI)
            load_xT(SECOND)

            def tile(t):
                nxt = t.following()
                rows = slice(t.tt * NT, (t.tt + 1) * NT)
                if exists(nxt.following()):
                    sp.wait_ge(z_mm, t.count(KI, KI))
                    sp.sem_inc(waited, 1)
                    sp.wait_ge(x_mm, nxt.count(KI, KI))
                    sp.sem_inc(waited, 1)
                    load_xT(nxt.following())
                sp.wait_ge(out_sb, t.count(SUB, 1))
                sp.sem_inc(waited, 1)
                sp.dma_start(x_nat[:], x[t.b, rows, :].rearrange("(s p) c -> p s c", p=P)).then_inc(x_in, 16)
                sp.wait_ge(ln_out, t.count(SUB, 2 * SUB))
                sp.sem_inc(waited, 1)
                sp.dma_start(x1[t.b, rows, :].rearrange("(s p) c -> p s c", p=P), res[:]).then_inc(x1_out, 16)

            with sp.Fori(0, BATCH - 1) as b:
                for tt in range(TILES_B):
                    tile(SeqTile(b, tt))
            for t in LAST_ROW:
                tile(t)
            sp.wait_ge(x1_out, 16 * TILES + 16)

        @block.tensor
        def _(pe):
            pe.wait_ge(weights_in, 16 * WEIGHTS)
            pe.wait_ge(consts, 2)
            pe.sem_inc(folded, 2)

            def x_product(t, j, k):
                if k == 0:
                    if j == 0:
                        pe.wait_ge(xT_in, t.count(16, 16))
                    if j >= 2:
                        pe.wait_ge(x_sb, t.count(KI, j - 1))
                    elif t is not OPENING:
                        pe.wait_ge(z_sb, SeqTile(t.b, t.tt - 1).count(KI, j + 3))
                last = pe.matmul(p_mm[j % 2][:], w_in[:, k, j * P:(j + 1) * P], xT_sb[t.tt % 2][:, k, :],
                                 start=k == 0, stop=k == KM - 1)
                if k == KM - 1:
                    last.then_inc(x_mm, 1)

            def z_product(t, j, k):
                if k == 0:
                    if j >= 2:
                        pe.wait_ge(z_sb, t.count(KI, j - 1))
                    else:
                        pe.wait_ge(rows_sb, t.count(2, 2))
                last = pe.matmul(p_mm[j % 2][:], w_in[:, k, DI + j * P:DI + (j + 1) * P], xT_sb[t.tt % 2][:, k, :],
                                 start=k == 0, stop=k == KM - 1)
                if k == KM - 1:
                    last.then_inc(z_mm, 1)

            def conv_product(t, j, k):
                if k == 0:
                    if j == 0:
                        pe.wait_ge(x_sb, t.count(KI, KI))
                    if j >= 2:
                        pe.wait_ge(conv_sb, t.count(KI, j - 1))
                    elif t is not OPENING:
                        pe.wait_ge(out_sb, SeqTile(t.b, t.tt - 1).count(SUB, 1))
                last = pe.matmul(p_mm[j % 2][:], w_conv[:, j, k, :], xb[:, j, k:k + NT],
                                 start=k == 0, stop=k == TAPS - 1)
                if k == TAPS - 1:
                    last.then_inc(conv_mm, 1)

            def front(t, i):
                par = t.tt % 2
                if i in CONV_SLOTS:
                    conv_product(t, *divmod(CONV_SLOTS.index(i), TAPS))
                elif i in Z_SLOTS:
                    z_product(t, *divmod(Z_SLOTS.index(i), KM))
                elif i in XD_SLOTS:
                    k = i - XD_SLOTS.start
                    if k == 0:
                        pe.wait_ge(conv_sb, t.count(KI, KI - 1))
                        pe.wait_ge(silu_u, t.count(1, 1))
                    last = pe.matmul(p_mm[0][0:DTR + 2 * NS, :], w_xp[:, k, :], uz[par][:, k, :],
                                     start=k == 0, stop=k == KI - 1)
                    if k == KI - 1:
                        last.then_inc(xd_mm, 1)
                elif i in ROWS_SLOTS:
                    m = ROWS_SLOTS.index(i)
                    if m == 0:
                        pe.wait_ge(conv_sb, t.count(KI, KI))
                        pe.wait_ge(xd_sb, t.count(1, 1))
                    pe.matmul(p_mm[1 - m][:], spread_bc[DTR:DTR + 2 * NS, m, :],
                              xd[DTR:DTR + 2 * NS, :], start=True, stop=True).then_inc(rows_mm, 1)
                elif i in DT_SLOTS:
                    c = DT_SLOTS.index(i)
                    if t is not OPENING or c:
                        pe.wait_ge(dt_sb, t.count(KI, c))
                    pe.matmul(p_dt[:], w_dt[:, c * P:(c + 1) * P], xd[0:DTR, :],
                              start=True, stop=True).then_inc(dt_mm, 1)

            def early(t, i):
                if i in X_SLOTS:
                    x_product(t, *divmod(X_SLOTS.index(i), KM))

            def place(g):
                chunk, quadrant, step = group_place(g)
                return chunk, quadrant // 2, (quadrant % 2) * 4 + step

            def spread_d(t, g):
                chunk, half, which = place(g)
                if g % GC == 0:
                    pe.wait_ge(d_lo, t.count(2 * KI, 2 * chunk + 2))
                if t is not OPENING or g >= 2:
                    pe.wait_ge(decay, t.count(NG, g - 1))
                pe.matmul(p_d[g % 2][:], pick_r[:, which, :], d_parts[:, half, chunk, :],
                          start=True, stop=True).then_inc(d_bc, 1)

            def spread_du(t, g):
                chunk, half, which = place(g)
                if g % GC == 0:
                    pe.wait_ge(du_lo, t.count(2 * KI, 2 * chunk + 2))
                pe.wait_ge(dub, t.count(NG, g + 1))
                pe.matmul(p_du[g % 2][:], pick_r[:, which, :], du_parts[:, half, chunk, :],
                          start=True, stop=True).then_inc(du_bc, 1)

            def fold_quad(t, q):
                chunk, step = divmod(q, 4)
                if step == 0:
                    pe.wait_ge(y_sb, t.count(KI, chunk + 1))
                pe.wait_ge(hc_done, t.count(NG, 4 * q + 4 + HRING))
                for k in range(4):
                    last = pe.matmul(p_y[32 * k:32 * k + 32, :], fold_w[:, step, :],
                                     hc[:, (4 * q + k) % HRING, :], start=step == 0, stop=step == 3,
                                     tile_position=(0, 32 * k))
                last.then_inc(folded, 1)

            def project(t, s, k_first, k_last):
                pe.wait_ge(gated, t.count(KI, k_last + 1))
                if k_first == 0:
                    if s < 2:
                        nxt = t.following()
                        if exists(nxt.following()):
                            pe.wait_ge(x_sb, nxt.following().count(KI, 3 + s))
                        elif exists(nxt):
                            pe.wait_ge(z_sb, nxt.count(KI, 3 + s))
                        else:
                            pe.wait_ge(out_sb, t.count(SUB, 1))
                    else:
                        pe.wait_ge(out_sb, t.count(SUB, s))
                zs = uz[t.tt % 2]
                for k in range(k_first, k_last + 1):
                    last = pe.matmul(p_mm[s % 2][:, 0:DM], zs[:, KI + k, s * P:(s + 1) * P],
                                     w_out[:, k, :], start=k == 0, stop=k == KI - 1)
                if k_last == KI - 1:
                    last.then_inc(out_mm, 1)

            for i in X_SLOTS:
                early(OPENING, i)
            for i in range(NG):
                if i >= NG - GC:
                    spread_du(OPENING, i - (NG - GC))
                for n in decays_of_slot(i):
                    if n >= NG:
                        spread_d(OPENING, n - NG)
                front(OPENING, i)
                early(SECOND, i)
                if i % 4 == 1 and GC + i - 8 >= NG:
                    fold_quad(OPENING, (GC + i - 8 - NG) // 4)

            def tile(t):
                nxt = t.following()
                for i in range(NG):
                    for spread, n in [(spread_du, GC + i)] + [(spread_d, n) for n in decays_of_slot(i)]:
                        now, g = at_group(t, n)
                        if exists(now):
                            spread(now, g)
                    if exists(nxt):
                        front(nxt, i)
                    if exists(nxt.following()):
                        early(nxt.following(), i)
                    for part in OUT_SLOTS.get(i, ()):
                        project(t, *part)
                    now, g = at_group(t, GC + i - 8)
                    if i % 4 == 1 and exists(now):
                        fold_quad(now, g // 4)

            with pe.Fori(0, BATCH - 1) as b:
                for tt in range(TILES_B):
                    tile(SeqTile(b, tt))
            for t in LAST_ROW:
                tile(t)

        @block.scalar
        def _(act):
            act.wait_ge(weights_in, 16 * WEIGHTS)
            act.preload_act_table_set(EXP_LN)
            act.activation(a_neg[:], a_neg[:], ACT.Exp).then_inc(a_exp, 1)
            act.wait_ge(consts, 2)
            act.wait_ge(zeroed, 1)
            act.activation(state[:], zeros[:], ACT.Copy).then_inc(saved, 16)

            def front(t, i):
                par = t.tt % 2
                for j in range(KI):
                    if i == Z_SLOTS[KM * j + KM - 1] + 1:
                        act.wait_ge(z_mm, t.count(KI, j + 1))
                        act.activation(uz[par][:, KI + j, :], p_mm[j % 2][:], ACT.Copy).then_inc(z_sb, 1)
                    if i == CONV_SLOTS[TAPS * j + TAPS - 1] + 1:
                        act.wait_ge(conv_mm, t.count(KI, j + 1))
                        act.activation(uz[par][:, j, :], p_mm[j % 2][:], ACT.Identity,
                                       bias=cb[:, j:j + 1]).then_inc(conv_sb, 1)
                if i == SILU_Z_SLOT:
                    act.wait_ge(z_sb, t.count(KI, KI))
                    act.activation(uz[par][:, KI:], uz[par][:, KI:], ACT.Silu).then_inc(silu_z, 1)
                    act.preload_act_table_set(EXP_LN)
                elif i == SILU_U_SLOT:
                    act.wait_ge(conv_sb, t.count(KI, KI))
                    act.activation(uz[par][:, 0:KI], uz[par][:, 0:KI], ACT.Silu).then_inc(silu_u, 1)
                    act.preload_act_table_set(EXP_LN)
                elif i == XD_SLOTS.stop:
                    act.wait_ge(xd_mm, t.count(1, 1))
                    act.activation(xd[:], p_mm[0][0:DTR + 2 * NS, :], ACT.Copy).then_inc(xd_sb, 1)
                elif i - 1 in ROWS_SLOTS:
                    m = ROWS_SLOTS.index(i - 1)
                    act.wait_ge(rows_mm, t.count(2, m + 1))
                    act.activation((b_rows, c_rows)[m][par][:], p_mm[1 - m][:], ACT.Copy).then_inc(rows_sb, 1)
                for c in range(KI):
                    k, step = c % 2, i - DT_SLOTS[c]
                    n = t.count(4 * KI, 4 * c)
                    x_ps = p_dt
                    if step == 1:
                        act.wait_ge(dt_mm, t.count(KI, c + 1))
                        if t is not OPENING or c > 1:
                            act.wait_ge(delta, t.count(KI, c - 1))
                            act.wait_ge(du_lo, t.count(2 * KI, 2 * c - 2))
                        act.activation(sp_e[k][:], x_ps[:], ACT.Abs, bias=dtb[:, c:c + 1]).then_inc(sp_act, 1)
                        act.wait_ge(sp_act, n + 1)
                        act.activation(sp_e[k][:], sp_e[k][:], ACT.Exp, scale=-1.0).then_inc(sp_act, 1)
                    elif step == 2:
                        act.wait_ge(sp_act, n + 2)
                        act.activation(sp_w[k][:], sp_e[k][:], ACT.Identity, bias=1.0).then_inc(sp_act, 1)
                        if t is not OPENING or c:
                            act.wait_ge(sp_dve, t.count(2 * KI, 2 * c))
                        act.activation(sp_l[:], sp_e[k][:], ACT.Ln, bias=1.0).then_inc(sp_act, 1)
                    elif step == 3:
                        act.activation(sp_r[k][:], x_ps[:], ACT.Relu, bias=dtb[:, c:c + 1]).then_inc(dt_sb, 1)
                    elif step == 7:
                        act.wait_ge(delta, t.count(KI, c + 1))
                        if t is not OPENING:
                            act.wait_ge(d_bc, t.count(NG, GC * (c + 1) - NG))
                        split_high(d_parts, sp_r[k], c, d_hi)
                    elif step == 9:
                        act.wait_ge(du, t.count(KI, c + 1))
                        if t is not OPENING:
                            act.wait_ge(du_bc, t.count(NG, GC * (c + 1) - NG))
                        split_high(du_parts, sp_w[k], c, du_hi)

            def early(t, i):
                if i == X_SLOTS[0]:
                    if t.tt == 0:
                        if t is not OPENING:
                            act.wait_ge(conv_mm, SeqTile(t.b, -1).count(KI, KI))
                        act.activation(xb[:, :, 0:TAPS - 1],
                                       zeros[:, 0:KI * (TAPS - 1)].rearrange("p (k w) -> p k w", k=KI),
                                       ACT.Copy).then_inc(halo, 1)
                    else:
                        act.wait_ge(conv_mm, SeqTile(t.b, t.tt - 1).count(KI, KI))
                        act.wait_ge(x_sb, SeqTile(t.b, t.tt - 1).count(KI, KI))
                        act.activation(xb[:, :, 0:TAPS - 1], xb[:, :, NT:NT + TAPS - 1],
                                       ACT.Copy).then_inc(halo, 1)
                for j in range(KI):
                    if i == X_SLOTS[KM * j + KM - 1] + 1:
                        act.wait_ge(halo, t.count(1, 1))
                        act.wait_ge(x_mm, t.count(KI, j + 1))
                        act.activation(xb[:, j, TAPS - 1:], p_mm[j % 2][:], ACT.Copy).then_inc(x_sb, 1)

            def split_high(parts, src, c, done):
                act.activation(parts[0:HALF, 0, c, :], src[0:HALF, :], ACT.Copy).then_inc(done, 1)
                act.activation(parts[HALF:P, 1, c, :], src[HALF:P, :], ACT.Copy).then_inc(done, 1)

            def decay_of(t, g):
                act.wait_ge(d_bc, t.count(NG, g + 1))
                act.wait_ge(scanned, t.count(NG, g + 1))
                act.activation(decays[:, g % DRING, :], p_d[g % 2][:], ACT.Exp,
                               scale=a_neg[:, g:g + 1]).then_inc(decay, 1)

            def save(t, q):
                act.wait_ge(scanned, t.count(NG, 4 * q + 4 + DRING))
                slot = (4 * q) % HRING
                src = (zeros[:, 0:4] if t.tt == TILES_B - 1 else
                       h[:, slot:slot + 4, NT - 1:NT].rearrange("p a b -> p (a b)"))
                act.activation(state[:, 4 * q:4 * q + 4], src, ACT.Copy).then_inc(saved, 1)

            for i in range(X_SLOTS[0], X_SLOTS[-1] + 2):
                early(OPENING, i)
            for i in range(NG):
                for n in decays_of_slot(i):
                    if n >= NG:
                        decay_of(OPENING, n - NG)
                if i % 4 == 2 and GC + i - 4 >= NG:
                    save(OPENING, (GC + i - 4 - NG) // 4)
                front(OPENING, i)
                early(SECOND, i)

            def tile(t):
                nxt = t.following()
                for i in range(NG):
                    for n in decays_of_slot(i):
                        now, g = at_group(t, n)
                        if exists(now):
                            decay_of(now, g)
                    now, g = at_group(t, GC + i - 4)
                    if i % 4 == 2 and exists(now):
                        save(now, g // 4)
                    if exists(nxt):
                        front(nxt, i)
                    if exists(nxt.following()):
                        early(nxt.following(), i)

            with act.Fori(0, BATCH - 1) as b:
                for tt in range(TILES_B):
                    tile(SeqTile(b, tt))
            for t in LAST_ROW:
                tile(t)

        @block.gpsimd
        def _(pool):
            pool.memset(zeros[:], 0.0).then_inc(zeroed, 1)
            pool.sem_inc(hc_done, HRING)

            def times_c(t, g):
                pool.wait_ge(scanned, t.count(NG, g + 1 + DRING))
                if g == 0:
                    pool.wait_ge(rows_sb, t.count(2, 2))
                if g % 4 == 0:
                    pool.wait_ge(folded, t.count(QUADS, g // 4 + 1))
                s = g % HRING
                pool.tensor_tensor(hc[:, s, :], h[:, s, :], c_rows[t.tt % 2][:], ALU.mult).then_inc(hc_done, 1)

            def front(t, i):
                for c in range(KI):
                    k = c % 2
                    if i == DT_SLOTS[c] + 5:
                        pool.wait_ge(sp_dve, t.count(2 * KI, 2 * c + 2))
                        pool.wait_ge(dt_sb, t.count(KI, c + 1))
                        pool.tensor_tensor(sp_r[k][:], sp_r[k][:], sp_e[k][:], ALU.subtract).then_inc(delta, 1)
                    elif i == DT_SLOTS[c] + 7:
                        pool.wait_ge(delta, t.count(KI, c + 1))
                        pool.wait_ge(silu_u, t.count(1, 1))
                        pool.tensor_tensor(sp_w[k][:], sp_r[k][:], uz[t.tt % 2][:, c, :],
                                           ALU.mult).then_inc(du, 1)

            def gate(t, c):
                pool.wait_ge(y_sb, t.count(KI, c + 1 + 1))
                pool.wait_ge(silu_z, t.count(1, 1))
                zs = uz[t.tt % 2]
                pool.tensor_tensor(zs[:, KI + c, :], zs[:, c, :], zs[:, KI + c, :], ALU.mult).then_inc(gated, 1)

            for i in range(NG):
                if GC + i - 1 >= NG:
                    times_c(OPENING, GC + i - 1 - NG)
                front(OPENING, i)

            def tile(t):
                nxt = t.following()
                for i in range(NG):
                    now, g = at_group(t, GC + i - 1)
                    if exists(now):
                        times_c(now, g)
                    if exists(nxt):
                        front(nxt, i)
                    if i % GC == 7:
                        gate(t, i // GC)

            with pool.Fori(0, BATCH - 1) as b:
                for tt in range(TILES_B):
                    tile(SeqTile(b, tt))
            for t in LAST_ROW:
                tile(t)

        @block.vector
        def _(dve):
            dve.wait_ge(weights_in, 16 * WEIGHTS)
            ident_sb = uz[1][:, 2, 0:P]
            dve.tensor_copy(pick_r[:], uz[1][:, 0:2, :].rearrange("p a (g m) -> p (a g) m", m=P))
            dve.tensor_copy(spread_bc[:], uz[1][:, 2, P:3 * P].rearrange("p (a m) -> p a m", m=P))
            for j in range(KI):
                for k in range(TAPS):
                    last = dve.tensor_scalar(w_conv[:, j, k, :], ident_sb, taps[:, j, k:k + 1], None, ALU.mult)
            last.then_inc(consts, 1)
            dve.wait_ge(a_exp, 1)
            dve.tensor_scalar(a_neg[:], a_neg[:], -1.0, None, ALU.mult).then_inc(consts, 1)
            dve.memset(res[:], 0.0).then_inc(out_sb, 1)
            dve.sem_inc(scanned, DRING)
            dve.sem_inc(dub, 2)
            dve.sem_inc(y_sb, 1)
            dve.sem_inc(x1_out, 16)

            def times_b(t, g):
                dve.wait_ge(du_bc, t.count(NG, g + 1))
                if g == 0:
                    dve.wait_ge(rows_sb, t.count(2, 2))
                dve.wait_ge(scanned, t.count(NG, g + 1 + DRING - DBRING))
                dve.tensor_tensor(db[:, g % DBRING, :], p_du[g % 2][:], b_rows[t.tt % 2][:],
                                  ALU.mult).then_inc(dub, 1)

            def scan(t, g):
                dve.wait_ge(decay, t.count(NG, g + 1))
                dve.wait_ge(dub, t.count(NG, g + 1 + 2))
                if g % 4 == 0:
                    dve.wait_ge(saved, t.count(QUADS, g // 4 + QUADS - 1))
                dve.wait_ge(hc_done, t.count(NG, g + 1))
                dve.tensor_tensor_scan(h[:, g % HRING, :], decays[:, g % DRING, :], db[:, g % DBRING, :], state[:, g:g + 1],
                                       ALU.mult, ALU.add).then_inc(scanned, 1)

            def front(t, i):
                par = t.tt % 2
                for c in range(KI):
                    k, step = c % 2, i - DT_SLOTS[c]
                    n = t.count(2 * KI, 2 * c)
                    if step == 3:
                        dve.wait_ge(sp_act, t.count(4 * KI, 4 * c + 4))
                        dve.scalar_tensor_tensor(out=sp_w[k][:], in0=sp_w[k][:], scalar=-1.0, in1=sp_l[:],
                                                 op0=ALU.add, op1=ALU.subtract).then_inc(sp_dve, 1)
                    elif step == 4:
                        dve.wait_ge(sp_dve, n + 1)
                        dve.scalar_tensor_tensor(out=sp_e[k][:], in0=sp_w[k][:], scalar=0.0, in1=sp_e[k][:],
                                                 op0=ALU.max, op1=ALU.subtract).then_inc(sp_dve, 1)
                    elif step == 8:
                        dve.wait_ge(d_hi, t.count(2 * KI, 2 * c + 2))
                        split_low(d_parts, sp_r[k], c, d_lo)
                    elif step == 10:
                        dve.wait_ge(du_hi, t.count(2 * KI, 2 * c + 2))
                        split_low(du_parts, sp_w[k], c, du_lo)

            def split_low(parts, src, c, done):
                dve.tensor_tensor(parts[HALF:P, 0, c, :], src[0:HALF, :],
                                  parts[0:HALF, 0, c, :].bitcast(F32), ALU.subtract).then_inc(done, 1)
                dve.tensor_tensor(parts[0:HALF, 1, c, :], src[HALF:P, :],
                                  parts[HALF:P, 1, c, :].bitcast(F32), ALU.subtract).then_inc(done, 1)

            def skip(t, c):
                u = uz[t.tt % 2][:, c, :]
                dve.wait_ge(folded, t.count(QUADS, 4 * c + 4 + 2))
                dve.scalar_tensor_tensor(out=u, in0=u, scalar=dpar[:, c:c + 1], in1=p_y[:],
                                         op0=ALU.mult, op1=ALU.add).then_inc(y_sb, 1)

            def residual(t, s):
                dve.wait_ge(out_mm, t.count(SUB, s + 1))
                if s == 0:
                    dve.wait_ge(x_in, t.count(16, 16))
                dve.tensor_tensor(res[:, s, :], p_mm[s % 2][:, 0:DM], x_nat[:, s, :], ALU.add).then_inc(out_sb, 1)

            N_LN = 2 * SUB + 1 + N_RSTD
            STATS_SLOT, AGGR_SLOT, RSTD_SLOT = 1, 5, 6
            SCALE_SLOT = 29

            def norm(t, i):
                def done(n):
                    dve.wait_ge(ln_dve, t.count(N_LN, n))

                if STATS_SLOT <= i < STATS_SLOT + SUB:
                    s = i - STATS_SLOT
                    if s == 0:
                        dve.wait_ge(out_sb, t.count(SUB, 1))
                    dve.bn_stats(stats[:, s, :], res[:, s, :]).then_inc(ln_dve, 1)
                elif i == AGGR_SLOT:
                    done(SUB)
                    dve.sem_inc(waited, 1)
                    for s in range(SUB):
                        dve.bn_aggr(mv[:, s, :], stats[:, s, :]).then_inc(ln_dve, 1)
                elif i == RSTD_SLOT:
                    done(2 * SUB)
                    dve.tensor_copy(var4[:], mv[:, :, 1:2].rearrange("p a b -> p (a b)")).then_inc(ln_dve, 1)
                elif RSTD_SLOT < i <= RSTD_SLOT + N_RSTD:
                    n = i - RSTD_SLOT - 1
                    done(2 * SUB + 1 + n)
                    rstd_step(dve, n, var4, y4, a4).then_inc(ln_dve, 1)
                elif SCALE_SLOT <= i < SCALE_SLOT + SUB:
                    s = i - SCALE_SLOT
                    done(N_LN)
                    dve.tensor_scalar(res[:, s, :], res[:, s, :], mv[:, s, 0:1], y4[:, s:s + 1],
                                      ALU.subtract, ALU.mult).then_inc(ln_out, 1)

            for i in range(NG):
                if i >= NG - GC:
                    times_b(OPENING, i - (NG - GC))
                if GC + i - 1 >= NG:
                    scan(OPENING, GC + i - 1 - NG)
                front(OPENING, i)

            def tile(t):
                nxt = t.following()
                for i in range(NG):
                    now, g = at_group(t, GC + i)
                    if exists(now):
                        times_b(now, g)
                    norm(t, i)
                    now, g = at_group(t, GC + i - 1)
                    if exists(now):
                        scan(now, g)
                    if exists(nxt):
                        front(nxt, i)
                    if i % GC == 6:
                        skip(t, i // GC)
                    if i in SUM_SLOTS:
                        if i == SUM_SLOTS[0]:
                            dve.wait_ge(ln_out, t.count(SUB, SUB))
                            dve.wait_ge(x1_out, t.count(16, 16))
                        residual(t, SUM_SLOTS.index(i))

            with dve.Fori(0, BATCH - 1) as b:
                for tt in range(TILES_B):
                    tile(SeqTile(b, tt))
            for t in LAST_ROW:
                tile(t)
            for i in range(SCALE_SLOT + SUB):
                norm(PAST, i)


W_COLS = (2 * KM + 2 * KH) * DH + KH * DM
W1_AT, W2_AT, H1_AT, H2_AT, W3_AT = 0, KM * DH, 2 * KM * DH, (2 * KM + KH) * DH, (2 * KM + 2 * KH) * DH


def ffn_stage(nc, sems, ctx, split, branch, weights, x1, scales, s3, ident, out):
    tag = "s_" if split else "g_"
    WT = F32R if split else F32
    parts = 2 if split else 1

    def sb(name, shape, dt=F32):
        return ctx.enter_context(nc.sbuf_tensor(tag + name, shape, dt))

    def sem(name):
        return sems.enter_context(nc.semaphore(tag + name))

    x_nat = [sb(f"x_nat{i}", [P, SUB, DM]) for i in range(2)]
    x_t = [[sb(f"x_t{i}{j}", [P, KM, NT], WT) for j in range(parts)] for i in range(2)]
    acts = [[sb(f"act{i}{j}", [P, KH, NT], WT) for j in range(parts)] for i in range(2)]
    hring = [sb(f"h{i}", [P, NT]) for i in range(3)] if split else None
    silu_t = [sb(f"silu{i}", [P, NT]) for i in range(2)]
    res = sb("res", [P, SUB, DM])
    sc = sb("sc", [P, 4, KH])
    s3b = sb("s3b", [P, DM])
    idn = sb("idn", [P, P])
    stats = sb("stats", [P, SUB, 6])
    mv = sb("mv", [P, SUB, 2])
    var4, y4, a4 = sb("var4", [P, SUB]), sb("y4", [P, SUB]), sb("a4", [P, SUB])
    bank = [ctx.enter_context(nc.psum_tensor(f"{tag}bank{i}", [P, NT], F32)) for i in range(8)]
    p_w1, p_w2, p_h, p_o = bank[0:2], bank[2:4], bank[4:6], bank[6:8]

    consts_in, stored = sem("consts_in"), sem("stored")
    x_in = [sem("x_in0"), sem("x_in1")]
    tr_mm, w1_mm, w2_mm, h_mm, o_mm = (sem(s) for s in ("tr_mm", "w1_mm", "w2_mm", "h_mm", "o_mm"))
    xt_hi, xt_lo = sem("xt_hi"), sem("xt_lo")
    silu, gate, gelu = sem("silu"), sem("gate"), sem("gelu")
    hi, lo = sem("hi"), sem("lo")
    scaled, summed = sem("scaled"), sem("summed")
    ln_dve, ln_out = sem("ln_dve"), sem("ln_out")
    waited = sem("waited")
    STEPS = TILES // PairTile.OF_STEP
    first = PairTile(0, 0)
    last_pair = [PairTile(STEPS - 1, tt) for tt in range(2)]

    def exists(t):
        return not isinstance(t.b, int) or t.b < STEPS

    L3 = 3 * KH

    block = ctx.enter_context(nc.Block())

    @block.sync
    def _(sp):
        def body():
            for k in range(4):
                sp.dma_start(sc[:, k, :], scales[k]).then_inc(consts_in, 16)
            sp.dma_start(s3b[:], s3).then_inc(consts_in, 16)
            sp.dma_start(idn[:], ident).then_inc(consts_in, 16)

            def load(t):
                row = t.b * (2 * NT) + t.tt * NT
                sp.dma_start(x_nat[t.tt][:], x1[bass.ds(row, NT), :].rearrange("(s p) c -> p s c", p=P))\
                  .then_inc(x_in[t.tt], 16)

            def tile(t):
                if exists(t.following()):
                    sp.wait_ge(summed, t.count(SUB, SUB))
                    sp.sem_inc(waited, 1)
                    load(t.following())
                sp.wait_ge(ln_out, t.count(SUB, SUB))
                sp.sem_inc(waited, 1)
                sp.dma_start(out[bass.ds(t.b * (2 * NT) + t.tt * NT, NT), :]
                             .rearrange("(s p) c -> p s c", p=P), res[:]).then_inc(stored, 16)

            load(first)
            with sp.Fori(0, STEPS - 1) as b:
                for tt in range(2):
                    tile(PairTile(b, tt))
            for t in last_pair:
                tile(t)
            sp.wait_ge(stored, 16 * TILES + 16)
        branch(sp, body)

    @block.tensor
    def _(pe):
        def body():
            pe.wait_ge(consts_in, 16 * 6)

            def product(dst, n_k, w_at, ins, rows_w, cols, wait=None):
                for k in range(n_k):
                    if wait:
                        wait(k)
                    for j in range(parts):
                        last = pe.matmul(dst, weights[:, w_at + k * rows_w + cols:w_at + k * rows_w + cols + P],
                                         ins[j][:, k, :], start=k == 0 and j == 0,
                                         stop=k == n_k - 1 and j == parts - 1)
                return last

            def transposes(t):
                pe.wait_ge(x_in[t.tt], t.b * 16 + 16)
                for k in range(KM):
                    if t is not first:
                        pe.wait_ge(scaled, PairTile(t.b, t.tt - 1).count(SUB, SUB))
                    for s in range(SUB):
                        last = pe.transpose(p_o[k][:, s * P:(s + 1) * P], x_nat[t.tt][:, s, k * P:(k + 1) * P],
                                            idn[:])
                    last.then_inc(tr_mm, 1)

            def gated(t):
                pe.wait_ge(xt_lo if split else xt_hi, t.count(KM, KM))
                for m in range(KH):
                    pe.wait_ge(silu, t.count(KH, m + 1))
                    product(p_w1[m % 2][:], KM, W1_AT, x_t[t.tt], DH, m * P).then_inc(w1_mm, 1)
                    pe.wait_ge(gate, t.count(KH, m + 1))
                    product(p_w2[m % 2][:], KM, W2_AT, x_t[t.tt], DH, m * P).then_inc(w2_mm, 1)

            def hidden(t, layer):
                w_at = (H1_AT, H2_AT)[layer]
                done = lo if split else (gate, gelu)[layer]

                def arrived(k):
                    if split:
                        pe.wait_ge(lo, t.count(L3, layer * KH + k + 1))
                    elif layer == 0:
                        pe.wait_ge(gate, t.count(KH, k + 1 + 2))
                    else:
                        pe.wait_ge(gelu, t.count(2 * KH, k + 1 + 2))
                for m in range(KH):
                    pe.wait_ge(gelu, t.count(2 * KH, layer * KH + m + 1))
                    product(p_h[m % 2][:], KH, w_at, acts[layer], DH, m * P,
                            arrived if m == 0 else None).then_inc(h_mm, 1)
                    if layer == 1 and m == 3 and exists(t.following()):
                        transposes(t.following())

            def output(t):
                for s in range(SUB):
                    if s < 2:
                        nxt = t.following() if exists(t.following()) else t
                        pe.wait_ge(xt_lo if split else xt_hi, nxt.count(KM, s + 1))
                    else:
                        pe.wait_ge(scaled, t.count(SUB, s - 1 + 4))
                    for k in range(KH):
                        if s == 0:
                            if split:
                                pe.wait_ge(lo, t.count(L3, 2 * KH + k + 1))
                            else:
                                pe.wait_ge(gelu, t.count(2 * KH, KH + k + 1 + 2))
                        for j in range(parts):
                            last = pe.matmul(p_o[s % 2][:, 0:DM], acts[0][j][:, k, s * P:(s + 1) * P],
                                             weights[:, W3_AT + k * DM:W3_AT + (k + 1) * DM],
                                             start=k == 0 and j == 0, stop=k == KH - 1 and j == parts - 1)
                    last.then_inc(o_mm, 1)

            def tile(t):
                hidden(t, 0)
                hidden(t, 1)
                output(t)
                if exists(t.following()):
                    gated(t.following())

            transposes(first)
            gated(first)
            with pe.Fori(0, STEPS - 1) as b:
                for tt in range(2):
                    tile(PairTile(b, tt))
            for t in last_pair:
                tile(t)
        branch(pe, body)

    @block.scalar
    def _(act):
        def body():
            act.wait_ge(consts_in, 16 * 6)
            act.sem_inc(silu, 2)
            act.sem_inc(gelu, 2)

            def transposed(t):
                for k in range(KM):
                    act.wait_ge(tr_mm, t.count(KM, k + 1))
                    act.activation(x_t[t.tt][0][:, k, :], p_o[k][:], ACT.Copy).then_inc(xt_hi, 1)

            def high(t, c):
                if c < KH:
                    act.wait_ge(gate, t.count(KH, c + 1 + 2))
                else:
                    act.wait_ge(gelu, t.count(2 * KH, c - KH + 1 + 2))
                act.activation(acts[(c // KH) % 2][0][:, c % KH, :], hring[c % 3][:], ACT.Copy).then_inc(hi, 1)

            def gated(t):
                for m in range(KH):
                    act.wait_ge(w1_mm, t.count(KH, m + 1))
                    if m > 1 or t is not first:
                        act.wait_ge(gate, t.count(KH, m - 2 + 1 + 2))
                    act.activation(silu_t[m % 2][:], p_w1[m % 2][:], ACT.Silu,
                                   scale=sc[:, 0, m:m + 1]).then_inc(silu, 1)
                    if split and m:
                        high(t, m - 1)
                if split:
                    high(t, KH - 1)

            def hidden(t, layer):
                for m in range(KH):
                    c = (layer + 1) * KH + m
                    act.wait_ge(h_mm, t.count(2 * KH, layer * KH + m + 1))
                    if split:
                        act.wait_ge(lo, t.count(L3, c - 2))
                        dst = hring[c % 3][:]
                    else:
                        dst = acts[1 - layer][0][:, m, :]
                    act.activation(dst, p_h[m % 2][:], ACT.Gelu,
                                   scale=sc[:, 2 + layer, m:m + 1]).then_inc(gelu, 1)
                    if split:
                        high(t, c)
                    if layer == 1 and m == 4 and exists(t.following()):
                        transposed(t.following())

            def tile(t):
                hidden(t, 0)
                hidden(t, 1)
                if exists(t.following()):
                    gated(t.following())

            transposed(first)
            gated(first)
            with act.Fori(0, STEPS - 1) as b:
                for tt in range(2):
                    tile(PairTile(b, tt))
            for t in last_pair:
                tile(t)
        branch(act, body)

    @block.vector
    def _(dve):
        def body():
            dve.wait_ge(consts_in, 16 * 6)
            dve.sem_inc(gate, 2)
            dve.sem_inc(scaled, 4)
            dve.sem_inc(summed, 4)
            dve.sem_inc(stored, 16)

            def transposed(t):
                if split:
                    for k in range(KM):
                        dve.wait_ge(xt_hi, t.count(KM, k + 1))
                        dve.tensor_tensor(x_t[t.tt][1][:, k, :], p_o[k][:], x_t[t.tt][0][:, k, :].bitcast(F32),
                                          ALU.subtract).then_inc(xt_lo, 1)

            def low(t, c):
                a = acts[(c // KH) % 2]
                dve.wait_ge(hi, t.count(L3, c + 1))
                dve.tensor_tensor(a[1][:, c % KH, :], hring[c % 3][:], a[0][:, c % KH, :].bitcast(F32),
                                  ALU.subtract).then_inc(lo, 1)

            def gated(t):
                for m in range(KH):
                    dve.wait_ge(w2_mm, t.count(KH, m + 1))
                    dve.wait_ge(silu, t.count(KH, m + 1 + 2))
                    if split and (m > 2 or t is not first):
                        dve.wait_ge(lo, t.count(L3, m - 2))
                    dst = hring[m % 3][:] if split else acts[0][0][:, m, :]
                    dve.scalar_tensor_tensor(out=dst, in0=p_w2[m % 2][:], scalar=sc[:, 1, m:m + 1],
                                             in1=silu_t[m % 2][:], op0=ALU.mult, op1=ALU.mult).then_inc(gate, 1)
                    if split and m:
                        low(t, m - 1)
                if split:
                    low(t, KH - 1)

            def hidden(t, layer):
                for m in range(KH):
                    if split:
                        low(t, (layer + 1) * KH + m)
                    if layer == 1 and m == 4 and exists(t.following()):
                        transposed(t.following())

            def residual(t):
                for s in range(SUB):
                    dve.wait_ge(o_mm, t.count(SUB, s + 1))
                    if s == 0:
                        dve.wait_ge(stored, t.count(16, 16))
                    dve.tensor_tensor(res[:, s, :], p_o[s % 2][:, 0:DM], s3b[:], ALU.mult).then_inc(scaled, 1)
                    dve.wait_ge(scaled, t.count(SUB, s + 1 + 4))
                    dve.tensor_tensor(res[:, s, :], res[:, s, :], x_nat[t.tt][:, s, :], ALU.add).then_inc(summed, 1)

            N_LN = 2 * SUB + 1 + 3 + 16

            def norm(t):
                count = [2 * SUB]

                def link(ins):
                    count[0] += 1
                    ins.then_inc(ln_dve, 1)
                    dve.wait_ge(ln_dve, t.count(N_LN, count[0]))

                dve.wait_ge(summed, t.count(SUB, SUB + 4))
                for s in range(SUB):
                    dve.bn_stats(stats[:, s, :], res[:, s, :]).then_inc(ln_dve, 1)
                dve.wait_ge(ln_dve, t.count(N_LN, SUB))
                dve.sem_inc(waited, 1)
                for s in range(SUB):
                    dve.bn_aggr(mv[:, s, :], stats[:, s, :]).then_inc(ln_dve, 1)
                dve.wait_ge(ln_dve, t.count(N_LN, 2 * SUB))
                link(dve.tensor_copy(var4[:], mv[:, :, 1:2].rearrange("p a b -> p (a b)")))
                for n in range(N_RSTD):
                    link(rstd_step(dve, n, var4, y4, a4))
                for s in range(SUB):
                    dve.tensor_scalar(res[:, s, :], res[:, s, :], mv[:, s, 0:1], y4[:, s:s + 1],
                                      ALU.subtract, ALU.mult).then_inc(ln_out, 1)

            def tile(t):
                hidden(t, 0)
                hidden(t, 1)
                residual(t)
                if exists(t.following()):
                    gated(t.following())
                norm(t)

            transposed(first)
            gated(first)
            with dve.Fori(0, STEPS - 1) as b:
                for tt in range(2):
                    tile(PairTile(b, tt))
            for t in last_pair:
                tile(t)
        branch(dve, body)


def weight_pieces(a):
    for name in ("w1T", "w2T", "h1T", "h2T", "w3T"):
        w = a[name]
        for k in range(w.shape[0] // P):
            yield w[k * P:(k + 1) * P, :]


def round_weights(nc, sems, ctx, a, flag):
    pieces = list(weight_pieces(a))
    n, ring = len(pieces), 12
    cols = [piece.shape[1] for piece in pieces]
    at = [sum(cols[:i]) for i in range(n)]
    weights = ctx.enter_context(nc.sbuf_tensor("weights_r", [P, W_COLS], F32R))
    with ExitStack() as own:
        stage = [own.enter_context(nc.sbuf_tensor(f"stage{i}", [P, DH], F32)) for i in range(ring)]
        lost = [own.enter_context(nc.sbuf_tensor(f"lost{i}", [P, DH], BF16)) for i in range(2)]
        ones = own.enter_context(nc.sbuf_tensor("ones", [P, P], BF16))
        losses = own.enter_context(nc.sbuf_tensor("losses", [P, 1], F32))
        total = own.enter_context(nc.psum_tensor("total", [P, NT], F32))
        loaded = [sems.enter_context(nc.semaphore(f"w_loaded{i}")) for i in range(ring)]
        ones_set, rounded, took, counted, summed, checked = (
            sems.enter_context(nc.semaphore(s)) for s in
            ("ones_set", "w_rounded", "w_took", "w_counted", "w_summed", "w_checked"))
        with nc.Block() as block:
            @block.sync
            def _(sp):
                for i, piece in enumerate(pieces):
                    if i >= ring:
                        sp.wait_ge(took, i - ring + 1)
                    sp.dma_start(stage[i % ring][:, 0:cols[i]], piece).then_inc(loaded[i % ring], 16)

            @block.scalar
            def _(act):
                for i in range(n):
                    act.wait_ge(loaded[i % ring], 16 * (i // ring + 1))
                    act.activation(weights[:, at[i]:at[i] + cols[i]], stage[i % ring][:, 0:cols[i]],
                                   ACT.Copy).then_inc(rounded, 1)

            @block.vector
            def _(dve):
                dve.memset(ones[:], 1.0).then_inc(ones_set, 1)
                for i in range(n):
                    dve.wait_ge(rounded, i + 1)
                    if i >= 2:
                        dve.wait_ge(counted, i - 1)
                    dve.tensor_tensor(lost[i % 2][:, 0:cols[i]], stage[i % ring][:, 0:cols[i]],
                                      weights[:, at[i]:at[i] + cols[i]].bitcast(F32),
                                      ALU.not_equal).then_inc(took, 1)
                dve.wait_ge(counted, n)
                dve.tensor_reduce(losses[0:1, :], total[0:1, :], mybir.AxisListType.X,
                                  ALU.max).then_inc(summed, 1)
                dve.wait_ge(summed, 1)
                dve.tensor_scalar(flag[0:1, 0:1], losses[0:1, :], 0.0, None,
                                  ALU.is_equal).then_inc(checked, 1)

            @block.tensor
            def _(pe):
                pe.wait_ge(ones_set, 1)
                for i in range(n):
                    pe.wait_ge(took, i + 1)
                    first_col = 0
                    while first_col < cols[i]:
                        width = min(NT, cols[i] - first_col)
                        last = pe.matmul(total[:, 0:width], ones[:], lost[i % 2][:, first_col:first_col + width],
                                         start=i == 0 and first_col == 0,
                                         stop=i == n - 1 and first_col + width == cols[i])
                        first_col += width
                    last.then_inc(counted, 1)
    return weights


def load_float32_weights(nc, sems, ctx, a, branch):
    weights = ctx.enter_context(nc.sbuf_tensor("weights_f32", [P, W_COLS], F32))
    loaded = sems.enter_context(nc.semaphore("weights_f32_in"))
    with nc.Block() as block:
        @block.sync
        def _(sp):
            def body():
                at = n = 0
                for piece in weight_pieces(a):
                    sp.dma_start(weights[:, at:at + piece.shape[1]], piece).then_inc(loaded, 16)
                    at += piece.shape[1]
                    n += 1
                sp.wait_ge(loaded, 16 * n)
            branch(sp, body)
    return weights


def program(nc, a, x1, out):
    with ExitStack() as sems:
        mamba_stage(nc, sems, a["xT"], a["x"], a["in_wT"], a["conv_w"], a["conv_b"], a["xp_wT"], a["dt_wT"],
                    a["dt_b"], a["A_log"], a["D_param"], a["out_wT"], a["pick"], a["fold"], a["ident"], x1)
        x1_rows, out_rows = (v.rearrange("b l c -> (b l) c") for v in (x1, out))
        scales = [a["s1"], a["s2"], a["sh1"], a["sh2"]]
        ident = a["ident"][:, 0:1, :].rearrange("p a m -> p (a m)")
        flag = sems.enter_context(nc.sbuf_tensor("flag", [P, 1], I32))

        def when(value):
            def branch(eng, body):
                exact = eng.value_load(flag[0:1, 0:1], min_val=0, max_val=1)
                with eng.If(exact == value):
                    body()
            return branch

        with ExitStack() as ctx:
            weights = round_weights(nc, sems, ctx, a, flag)
            ffn_stage(nc, sems, ctx, True, when(1), weights, x1_rows, scales, a["s3"], ident, out_rows)
        with ExitStack() as ctx:
            weights = load_float32_weights(nc, sems, ctx, a, when(0))
            ffn_stage(nc, sems, ctx, False, when(0), weights, x1_rows, scales, a["s3"], ident, out_rows)


def shape_constants():
    pick = np.zeros((P, HALF // GD, P), np.float32)
    fold = np.zeros((P, 4, 32), np.float32)
    ident = np.zeros((P, 3, P), np.float32)
    ident[:, 0] = np.eye(P)
    for d in range(GD):
        for n in range(NS):
            row = d * NS + n
            for which in range(HALF // GD):
                pick[which * GD + d, which, row] = 1
                pick[HALF + which * GD + d, which, row] = 1
            for step in range(4):
                fold[row, step, step * GD + d] = 1
            ident[DTR + n, 1, row] = 1
            ident[DTR + NS + n, 2, row] = 1
    return pick, fold, ident


def kernel(**inputs):
    import concourse.bacc as bacc
    from concourse.bass_utils import run_bass_kernel_spmd

    v = {k.removeprefix("L0_"): np.asarray(x) for k, x in inputs.items()}
    pick, fold, ident = shape_constants()

    def column(x):
        return np.ascontiguousarray(x.reshape(-1, P).T)

    a_log = v["attn_A_log"].reshape(KI, 4, 4, GD, NS).transpose(3, 4, 0, 2, 1).reshape(P, NG)
    arrays = {
        "x": v["attn_hidden_states"],
        "xT": v["attn_hidden_states"].transpose(0, 2, 1),
        "in_wT": v["attn_in_proj_w"].T, "conv_w": v["attn_conv_w"], "conv_b": column(v["attn_conv_b"]),
        "xp_wT": v["attn_x_proj_w"].T, "dt_wT": v["attn_dt_proj_w"].T, "dt_b": column(v["attn_dt_proj_b"]),
        "A_log": a_log, "D_param": column(v["attn_D_param"]), "out_wT": v["attn_out_proj_w"].T,
        "pick": pick, "fold": fold, "ident": ident,
        "w1T": v["ffn_w1_w"].T, "w2T": v["ffn_w2_w"].T, "h1T": v["ffn_h1_w"].T, "h2T": v["ffn_h2_w"].T,
        "w3T": v["ffn_w3_w"].T,
        "s1": column(v["ffn_w1_s"]), "s2": column(v["ffn_w2_s"]), "sh1": column(v["ffn_h1_s"]),
        "sh2": column(v["ffn_h2_s"]), "s3": np.broadcast_to(v["ffn_w3_s"], (P, DM)),
    }
    arrays = {k: np.ascontiguousarray(x) for k, x in arrays.items()}
    nc = bacc.Bacc("TRN2", target_bir_lowering=False, num_devices=1)
    aps = {k: nc.dram_tensor(f"in_{k}", x.shape, mybir.dt.from_np(x.dtype), kind="ExternalInput").ap()
           for k, x in arrays.items()}
    x1 = nc.dram_tensor("x1", (BATCH, SEQ, DM), F32, kind="Internal").ap()
    out = nc.dram_tensor("out", (BATCH, SEQ, DM), F32, kind="ExternalOutput").ap()
    program(nc, aps, x1, out)
    r = run_bass_kernel_spmd(nc, [{f"in_{k}": x for k, x in arrays.items()}], core_ids=[0])
    return r.results[0]["out"]
```
